# Optimizing a Trainium2 kernel written in Bass

```python
import numpy as np
import jax
import jax.numpy as jnp

def _softmax(x, axis=-1):
    return jax.nn.softmax(x, axis=axis)

def _gelu(x):
    return jax.nn.gelu(x, approximate=True)

def _silu(x):
    return jax.nn.silu(x)

def _sigmoid(x):
    return jax.nn.sigmoid(x)

def _layernorm(x, axis=-1, eps=1e-05):
    m = jnp.mean(x, axis=axis, keepdims=True)
    v = jnp.var(x, axis=axis, keepdims=True)
    return (x - m) / jnp.sqrt(v + eps)

def _scatter_add(tgt, idx, src, axis=0):
    return tgt.at[idx].add(src)

def _segment_sum(src, seg, n):
    return jax.ops.segment_sum(src, seg, n)
kernel_name = 'mk_cond_seq_d1_seqx_r4_a1ac83'

def setup_inputs(seed: int=0):
    np.random.seed(seed)
    _w = jnp.asarray

    def _rec_inputs():
        import jax
        import jax.numpy as jnp
        _rk = jax.random.key(seed)
        x = -0.0002928 + 1 * jax.random.normal(jax.random.fold_in(_rk, 1), (8, 512, 256), jnp.float32)
        _lenS = 512 - jax.random.randint(jax.random.fold_in(_rk, 7), (8,), 0, max(1, 512 // 4) + 1, jnp.int32)
        _lenS2 = 512 - jax.random.randint(jax.random.fold_in(_rk, 8), (8,), 0, max(1, 512 // 4) + 1, jnp.int32)
        cond_1024 = 0.000887014 + 1.03683 * jax.random.normal(jax.random.fold_in(_rk, 11), (8, 256), jnp.float32)
        return (x, cond_1024)
    x, cond_1024 = _rec_inputs()

    def _L0_cond_setup():
        import math
        import jax, jax.numpy as jnp
        import numpy as np
        D_MODEL = 256
        N_HEADS = 16
        FFN_DIM = 1024
        EPS = 1e-05

        def _layernorm(x, w, b):
            mu = jnp.mean(x, axis=-1, keepdims=True)
            var = jnp.var(x, axis=-1, keepdims=True)
            return (x - mu) * jax.lax.rsqrt(var + EPS) * w + b

        def _modulate(x, shift, scale):
            return x * (1.0 + scale[:, None, :]) + shift[:, None, :]
        key = jax.random.key(seed)
        ks = jax.random.split(key, 16)
        B, S, D, F = (2, 512, D_MODEL, FFN_DIM)
        s = 0.02
        return {'x': jax.random.normal(ks[0], (B, S, D), jnp.float32), 't_emb': jax.random.normal(ks[1], (B, D), jnp.float32), 'ln1_w': jnp.ones((D,), jnp.float32), 'ln1_b': jnp.zeros((D,), jnp.float32), 'ln2_w': jnp.ones((D,), jnp.float32), 'ln2_b': jnp.zeros((D,), jnp.float32), 'wq': jax.random.normal(ks[2], (D, D), jnp.float32) * s, 'bq': jnp.zeros((D,), jnp.float32), 'wk': jax.random.normal(ks[3], (D, D), jnp.float32) * s, 'bk': jnp.zeros((D,), jnp.float32), 'wv': jax.random.normal(ks[4], (D, D), jnp.float32) * s, 'bv': jnp.zeros((D,), jnp.float32), 'wo': jax.random.normal(ks[5], (D, D), jnp.float32) * s, 'bo': jnp.zeros((D,), jnp.float32), 'wt_attn': jax.random.normal(ks[6], (D, 2 * D), jnp.float32) * s, 'bt_attn': jnp.zeros((2 * D,), jnp.float32), 'wt_ffn': jax.random.normal(ks[7], (D, 2 * D), jnp.float32) * s, 'bt_ffn': jnp.zeros((2 * D,), jnp.float32), 'w1': jax.random.normal(ks[8], (D, F), jnp.float32) * s, 'b1': jnp.zeros((F,), jnp.float32), 'w2': jax.random.normal(ks[9], (F, D), jnp.float32) * s, 'b2': jnp.zeros((D,), jnp.float32)}
    _L0_cond_all = _L0_cond_setup()
    _L0_cond_in = {k: v for k, v in _L0_cond_all.items() if k in ('ln1_w', 'ln1_b', 'ln2_w', 'ln2_b', 'wq', 'bq', 'wk', 'bk', 'wv', 'bv', 'wo', 'bo', 'wt_attn', 'bt_attn', 'wt_ffn', 'bt_ffn', 'w1', 'b1', 'w2', 'b2')}
    del _L0_cond_all
    return {'x': x, 'cond_1024': cond_1024, 'L0_cond_ln1_w': _L0_cond_in['ln1_w'], 'L0_cond_ln1_b': _L0_cond_in['ln1_b'], 'L0_cond_ln2_w': _L0_cond_in['ln2_w'], 'L0_cond_ln2_b': _L0_cond_in['ln2_b'], 'L0_cond_wq': _L0_cond_in['wq'], 'L0_cond_bq': _L0_cond_in['bq'], 'L0_cond_wk': _L0_cond_in['wk'], 'L0_cond_bk': _L0_cond_in['bk'], 'L0_cond_wv': _L0_cond_in['wv'], 'L0_cond_bv': _L0_cond_in['bv'], 'L0_cond_wo': _L0_cond_in['wo'], 'L0_cond_bo': _L0_cond_in['bo'], 'L0_cond_wt_attn': _L0_cond_in['wt_attn'], 'L0_cond_bt_attn': _L0_cond_in['bt_attn'], 'L0_cond_wt_ffn': _L0_cond_in['wt_ffn'], 'L0_cond_bt_ffn': _L0_cond_in['bt_ffn'], 'L0_cond_w1': _L0_cond_in['w1'], 'L0_cond_b1': _L0_cond_in['b1'], 'L0_cond_w2': _L0_cond_in['w2'], 'L0_cond_b2': _L0_cond_in['b2']}

def reference(x, cond_1024, L0_cond_ln1_w, L0_cond_ln1_b, L0_cond_ln2_w, L0_cond_ln2_b, L0_cond_wq, L0_cond_bq, L0_cond_wk, L0_cond_bk, L0_cond_wv, L0_cond_bv, L0_cond_wo, L0_cond_bo, L0_cond_wt_attn, L0_cond_bt_attn, L0_cond_wt_ffn, L0_cond_bt_ffn, L0_cond_w1, L0_cond_b1, L0_cond_w2, L0_cond_b2):
    import jax
    import jax.numpy as jnp

    def _L0_cond_ref(x, t_emb, ln1_w, ln1_b, ln2_w, ln2_b, wq, bq, wk, bk, wv, bv, wo, bo, wt_attn, bt_attn, wt_ffn, bt_ffn, w1, b1, w2, b2):
        import math
        import jax, jax.numpy as jnp
        import numpy as np
        D_MODEL = 256
        N_HEADS = 16
        FFN_DIM = 1024
        EPS = 1e-05

        def _layernorm(x, w, b):
            mu = jnp.mean(x, axis=-1, keepdims=True)
            var = jnp.var(x, axis=-1, keepdims=True)
            return (x - mu) * jax.lax.rsqrt(var + EPS) * w + b

        def _modulate(x, shift, scale):
            return x * (1.0 + scale[:, None, :]) + shift[:, None, :]
        B, S, D = x.shape
        H = N_HEADS
        hd = D // H
        residual = x
        xn = _layernorm(x, ln1_w, ln1_b)
        t_attn = t_emb @ wt_attn + bt_attn
        shift_a, scale_a = jnp.split(t_attn, 2, axis=-1)
        xn = _modulate(xn, shift_a, scale_a)
        q = (xn @ wq + bq).reshape(B, S, H, hd).transpose(0, 2, 1, 3)
        k = (xn @ wk + bk).reshape(B, S, H, hd).transpose(0, 2, 1, 3)
        v = (xn @ wv + bv).reshape(B, S, H, hd).transpose(0, 2, 1, 3)
        scores = jnp.einsum('bhqd,bhkd->bhqk', q, k) / math.sqrt(hd)
        attn = jax.nn.softmax(scores, axis=-1)
        out = jnp.einsum('bhqk,bhkd->bhqd', attn, v)
        out = out.transpose(0, 2, 1, 3).reshape(B, S, D)
        x = residual + (out @ wo + bo)
        residual = x
        xn = _layernorm(x, ln2_w, ln2_b)
        t_ffn = t_emb @ wt_ffn + bt_ffn
        shift_f, scale_f = jnp.split(t_ffn, 2, axis=-1)
        xn = _modulate(xn, shift_f, scale_f)
        h = jax.nn.gelu(xn @ w1 + b1, approximate=False)
        x = residual + (h @ w2 + b2)
        return x
    x = _L0_cond_ref(x, cond_1024, L0_cond_ln1_w, L0_cond_ln1_b, L0_cond_ln2_w, L0_cond_ln2_b, L0_cond_wq, L0_cond_bq, L0_cond_wk, L0_cond_bk, L0_cond_wv, L0_cond_bv, L0_cond_wo, L0_cond_bo, L0_cond_wt_attn, L0_cond_bt_attn, L0_cond_wt_ffn, L0_cond_bt_ffn, L0_cond_w1, L0_cond_b1, L0_cond_w2, L0_cond_b2)
    return x

_drawn_inputs = setup_inputs


def setup_inputs(seed=0):
    import zlib

    import numpy as np

    out = dict(_drawn_inputs(seed))
    spreads = {'L0_cond_ln1_w': (1.0, 0.6),
     'L0_cond_ln1_b': (0.0, 0.727),
     'L0_cond_ln2_w': (1.0, 0.6),
     'L0_cond_ln2_b': (0.0, 0.728),
     'L0_cond_bq': (0.0, 0.8),
     'L0_cond_bk': (0.0, 0.8),
     'L0_cond_bv': (0.0, 0.271),
     'L0_cond_bo': (0.0, 0.1),
     'L0_cond_bt_attn': (0.0, 0.75),
     'L0_cond_bt_ffn': (0.0, 0.483),
     'L0_cond_b1': (0.0, 0.1),
     'L0_cond_b2': (0.0, 0.1)}
    factors = {'L0_cond_wq': 8.0, 'L0_cond_wk': 8.0}
    for name, (base, spread) in spreads.items():
        noise = np.random.default_rng([zlib.crc32(name.encode()), seed]).standard_normal(out[name].shape)
        drawn = base * np.exp(spread * noise) if base else spread * noise
        out[name] = jnp.asarray(drawn.astype(out[name].dtype))
    for name, factor in factors.items():
        out[name] = (out[name] * factor).astype(out[name].dtype)
    return out
```

```python
from contextlib import ExitStack

import concourse.bass as bass
from concourse import mybir

F32 = mybir.dt.float32
F32R = mybir.dt.float32r
ALU = mybir.AluOpType
ACT = mybir.ActivationFunctionType
AX = mybir.AxisListType

P = 128
N_HEADS = 16
EPS = 1e-5


def cond_transformer_block(nc, x, cond, ln1_w, ln1_b, ln2_w, ln2_b, wq, bq, wk, bk, wv, bv, wo, bo,
                           wt_attn, bt_attn, wt_ffn, bt_ffn, w1, b1, w2, b2, out):
    B, S, D = x.shape
    F = w1.shape[1]
    HD = D // N_HEADS
    T = S // P
    C = D // P
    FT = F // P
    G = 4
    UB = N_HEADS // G
    UNITS = B * UB
    TILES = G * T
    LAG = 2
    K_A = 4 * HD + 1
    K_B = K_A + 2
    VH = HD + 1
    VW = 32
    TV = 9
    HB = 4
    assert S == 512 and D == 256 and HD == 16 and F == 1024

    with ExitStack() as ctx:
        def sb(name, shape, dt=F32):
            return ctx.enter_context(nc.sbuf_tensor(name, shape, dt))

        def sem(name):
            return ctx.enter_context(nc.semaphore(name))

        resid = sb("resid", [P, B, T, D])
        wqkv = {}
        for n in ("q", "k", "v", "o"):
            wqkv[n] = (sb(f"w{n}_hi", [P, C, D], F32R), sb(f"w{n}_lo", [P, C, D], F32R))
        w1_hi, w1_lo = sb("w1_hi", [P, C, F], F32R), sb("w1_lo", [P, C, F], F32R)
        w2_hi, w2_lo = sb("w2_hi", [P, FT, D], F32R), sb("w2_lo", [P, FT, D], F32R)
        q_stack = sb("q_stack", [P, UB, G, S], F32R)
        k_stack = sb("k_stack", [P, UB, G, S], F32R)
        probs = sb("probs", [P, 2, G, S])
        v_ones = sb("v_ones", [P, T, VH * N_HEADS + VW - VH])
        xhat = sb("xhat", [P, T, D])
        xm_hi, xm_lo = sb("xm_hi", [P, C, S], F32R), sb("xm_lo", [P, C, S], F32R)
        q_hi, q_lo = sb("q_hi", [P, S], F32R), sb("q_lo", [P, S])
        k_hi, k_lo = sb("k_hi", [P, S], F32R), sb("k_lo", [P, S])
        pv_sb = sb("pv_sb", [P, S])
        attn = sb("attn", [P, T, D])
        at_hi, at_lo = sb("at_hi", [P, C, S // 2], F32R), sb("at_lo", [P, C, S // 2], F32R)
        bo_eff = sb("bo_eff", [P, B, D])
        b2_bc = sb("b2_bc", [P, D])
        ident = sb("ident", [P, P])
        neg_max = sb("neg_max", [P, 2, TILES])
        m_hi, m_lo = sb("m_hi", [TILES, P], F32R), sb("m_lo", [TILES, P], F32R)
        recip = sb("recip", [P, T, G])
        stats = sb("stats", [P, T, 6])
        mean_var = sb("mean_var", [P, T, 2])
        rstd, eps, expo = sb("rstd", [P, T]), sb("eps", [P, T]), sb("expo", [P, T])
        n_vec = 4 * C + C + 2 * 2 * C + FT
        vec_cols = sb("vec_cols", [P, n_vec + 2 * C])
        cond_cols = sb("cond_cols", [P, C, B])
        mod = sb("mod", [P, 2, 2 * C, B])
        gain = sb("gain", [P, 2, C, B])
        offs = sb("offs", [P, 2, C, B])
        offs_hi, offs_lo = sb("offs_hi", [P, C, B], F32R), sb("offs_lo", [P, C, B], F32R)
        qk_bias = sb("qk_bias", [P, 2 * C, B])
        v_bias = sb("v_bias", [P, C, B])
        b1_eff = sb("b1_eff", [P, FT, B])
        gain_now = sb("gain_now", [P, 2, C])
        qk_bias_now = sb("qk_bias_now", [P, 2 * C])
        b1_now = sb("b1_now", [P, 2, FT])

        w_raw = resid[:, 4:6, :, :].rearrange("p b t d -> p (b t) d").rearrange("p (n c) d -> p n c d", c=C)
        wt_raw = resid[:, 6:8, :, :].rearrange("p b t d -> p b (t d)").rearrange("p n (c f) -> p n c f", c=C)
        vec_rows, qk_rows, qk_rows_p = attn[0:n_vec, 0, 0:P], attn[0:2 * C, 1, 0:P], attn[0:2 * C, 2, 0:P]
        cond_rows = attn[0:B, 3, :]
        bo_bc = pv_sb[:, 0:D]
        probs_flat = probs[:, :, :, :].rearrange("p a g s -> p (a g s)")
        w1_raw = probs_flat[:, 0:C * F].rearrange("p (c f) -> p c f", c=C)
        w2_raw = probs_flat[:, C * F:C * F + FT * D].rearrange("p (f d) -> p f d", f=FT)
        h_full = probs[:, 0, :, :]
        h_hi = q_stack[:, 0, :, :]
        h_lo = q_stack[:, 1, :, :]
        ym = [(xm_hi[:, :, :], xm_lo[:, :, :]), (k_stack[:, 0, 0:C, :], k_stack[:, 1, 0:C, :])]

        scores = [ctx.enter_context(nc.psum_tensor(f"scores{n}", [P, S], F32)) for n in range(3)]
        shifted = [ctx.enter_context(nc.psum_tensor(f"shifted{n}", [P, S], F32)) for n in range(2)]
        pv = ctx.enter_context(nc.psum_tensor("pv", [P, S], F32))
        turn = ctx.enter_context(nc.psum_tensor("turn", [P, S], F32))
        work = ctx.enter_context(nc.psum_tensor("work", [P, S], F32))

        sums = [shifted, (scores[2], pv)]

        x_in = [sem("x0_in"), sem("x1_in"), sem("x4_in")]
        vec_in, cond_in, wt_in, raw_in = sem("vec_in"), sem("cond_in"), sem("wt_in"), sem("raw_in")
        mlp_in, bc_in, qk_rows_in = sem("mlp_in"), sem("bc_in"), sem("qk_rows_in")
        ident_zero, ident_ok, consts_ok = sem("ident_zero"), sem("ident_ok"), sem("consts_ok")
        rows_turned, cols_ok, mod_mm, mod_step = sem("rows_turned"), sem("cols_ok"), sem("mod_mm"), sem("mod_step")
        rows_perm = sem("rows_perm")
        bias_mm, bias_ok, u_mm, u_ok = sem("bias_mm"), sem("bias_ok"), sem("u_mm"), sem("u_ok")
        w_hi_ok, w_lo_ok, mlp_hi_ok, mlp_lo_ok = sem("w_hi_ok"), sem("w_lo_ok"), sem("mlp_hi_ok"), sem("mlp_lo_ok")
        stack_in = [sem("stack_even_in"), sem("stack_odd_in")]
        max_in = [sem("max_even_in"), sem("max_odd_in")]
        scores_ok, shifted_ok, pv_ok = sem("scores_ok"), sem("shifted_ok"), sem("pv_ok")
        max_turned, pv_turned = sem("max_turned"), sem("pv_turned")
        qk_mm, v_mm, x_turned, attn_turned, wo_mm = (sem("qk_mm"), sem("v_mm"), sem("x_turned"),
                                                     sem("attn_turned"), sem("wo_mm"))
        max_ok, m_lo_ok, qk_lo_ok, xm_lo_ok = sem("max_ok"), sem("m_lo_ok"), sem("qk_lo_ok"), sem("xm_lo_ok")
        recip_ok, attn_ok, at_lo_ok, x1_ok = sem("recip_ok"), sem("attn_ok"), sem("at_lo_ok"), sem("x1_ok")
        bn_ok, stats_ok, xhat_ok = sem("bn_ok"), sem("stats_ok"), sem("xhat_ok")
        gain_ok, qk_bias_ok, gain2_ok, b1_ok = sem("gain_ok"), sem("qk_bias_ok"), sem("gain2_ok"), sem("b1_ok")
        exp_ok, m_hi_ok, qk_ok, xm_hi_ok = sem("exp_ok"), sem("m_hi_ok"), sem("qk_ok"), sem("xm_hi_ok")
        pv_sb_ok, at_hi_ok, v_ok = sem("pv_sb_ok"), sem("at_hi_ok"), sem("v_ok")
        var_eps_ok, rstd_ok, resid_ok = sem("var_eps_ok"), sem("rstd_ok"), sem("resid_ok")
        bn2_ok, stats2_ok, xhat2_ok = sem("bn2_ok"), sem("stats2_ok"), sem("xhat2_ok")
        var_eps2_ok, rstd2_ok = sem("var_eps2_ok"), sem("rstd2_ok")
        resid2_ok, x2_turned, ym_hi_ok, ym_lo_ok = (sem("resid2_ok"), sem("x2_turned"), sem("ym_hi_ok"),
                                                    sem("ym_lo_ok"))
        w1_mm, h_hi_ok, h_ok, h_lo_ok, w2_mm, y_ok, stored = (sem("w1_mm"), sem("h_hi_ok"), sem("h_ok"),
                                                              sem("h_lo_ok"), sem("w2_mm"), sem("y_ok"),
                                                              sem("stored"))

        x_v = x.rearrange("b (p t) d -> p b (t d)", t=T)
        out_v = out.rearrange("b (p t) d -> p b (t d)", t=T)

        def live(n, end):
            return not isinstance(n, int) or 0 <= n < end

        def wait(eng, s, value):
            if not isinstance(value, int) or value > 0:
                eng.wait_ge(s, value)

        def over_batches(eng, body):
            body(0)
            with eng.Fori(1, B - 1) as i:
                body(i)
            body(B - 1)
            body(B)

        def over_mlp_batches(eng, body):
            body(0, 0)
            with eng.Fori(0, B // 2 - 1) as k:
                body(2 * k + 1, 1)
                body(2 * k + 2, 0)
            body(B - 1, 1)
            body(B, 0)

        at = {}
        row = 0
        vectors = [("ln1_w", ln1_w, C), ("ln1_b", ln1_b, C), ("ln2_w", ln2_w, C), ("ln2_b", ln2_b, C),
                   ("bv", bv, C), ("bt_attn", bt_attn, 2 * C), ("bt_ffn", bt_ffn, 2 * C), ("b1", b1, FT)]
        for name, _, n in vectors:
            at[name] = row
            row += n
        assert row == n_vec

        def by_head_in_unit(ap):
            return ap.rearrange("p (u h d) -> p u d h", u=2, h=G)

        def in_order(ap):
            return ap.rearrange("p (u d h) -> p u d h", u=2, h=G)

        block = ctx.enter_context(nc.Block())

        @block.sync
        def _(sp):
            sp.dma_start(cond_rows, cond).then_inc(cond_in, 16)
            for name, v, n in vectors:
                sp.dma_start(attn[at[name]:at[name] + n, 0, 0:P],
                             v.rearrange("(n p) -> n p", p=P)).then_inc(vec_in, 16)
            sp.dma_start(attn[0:C, 1, 0:P], bq.rearrange("(n p) -> n p", p=P)).then_inc(qk_rows_in, 16)
            sp.dma_start(attn[C:2 * C, 1, 0:P], bk.rearrange("(n p) -> n p", p=P)).then_inc(qk_rows_in, 16)
            sp.dma_start(resid[:, 0, :, :], x_v[:, 0, :].rearrange("p (t d) -> p t d", t=T)).then_inc(x_in[0], 16)
            for n, w in enumerate((wq, wk, wv, wo)):
                sp.dma_start(w_raw[:, n, :, :], w.rearrange("(c p) f -> p c f", p=P)).then_inc(raw_in, 16)
            sp.dma_start(resid[:, 1:4, :, :],
                         x_v[:, 1:4, :].rearrange("p b (t d) -> p b t d", t=T)).then_inc(x_in[1], 16)

            def batch(i):
                for g in range(UB):
                    u = UB * i + g + 1
                    slot, m = (g + 1) % UB, ((g + 1) % UB) // 2
                    if live(u, UNITS):
                        load_stacks(u, slot, i if g + 1 < UB else i + 1, m)
                    if live(u - 2, UNITS):
                        load_max(u - 2, (g - 1) % UB)

            def load_stacks(u, slot, b, m):
                split, freed = 4 * b + 2 * m + 2, TILES * (u - UB + 1)
                if not isinstance(u, int):
                    split, freed = sp.to_reg(split), sp.to_reg(freed)
                wait(sp, qk_lo_ok, split)
                wait(sp, shifted_ok, freed)
                if isinstance(u, int) and u < UB:
                    wait(sp, consts_ok, 1)
                rows = slice(64 * (slot % 2), 64 * (slot % 2) + 64)
                qh, kh = q_hi[:, :].bitcast(F32), k_hi[:, :].bitcast(F32)
                for stack, parts in ((q_stack, (qh, qh, q_lo, q_lo)), (k_stack, (kh, k_lo, kh, k_lo))):
                    for n, part in enumerate(parts):
                        sp.dma_start(stack[HD * n:HD * n + HD, slot, :, :].bitcast(F32),
                                     part[rows, :]).then_inc(stack_in[slot % 2], 16)

            def load_max(u, slot):
                wait(sp, m_lo_ok, u + 1)
                for n, part in enumerate((m_hi, m_lo)):
                    sp.dma_start(q_stack[K_A + n:K_A + n + 1, slot, :, :].bitcast(F32),
                                 part[:, :].bitcast(F32)).then_inc(max_in[slot % 2], 16)

            load_stacks(0, 0, 0, 0)
            sp.wait_ge(bias_ok, 3)
            sp.wait_ge(u_ok, B + 1)
            sp.wait_ge(w_lo_ok, 4)
            sp.dma_start(resid[:, 4:B, :, :],
                         x_v[:, 4:B, :].rearrange("p b (t d) -> p b t d", t=T)).then_inc(x_in[2], 16)
            over_batches(sp, batch)

        def one(i):
            return slice(i, i + 1) if isinstance(i, int) else bass.ds(i, 1)

        @block.gpsimd
        def _(pool):
            pool.memset(ident[:, :], 0.0).then_inc(ident_zero, 1)
            pool.wait_ge(ident_zero, 1)
            pool.affine_select(out=ident[:, :], in_=ident[:, :], compare_op=ALU.not_equal, fill=1.0, base=0,
                               pattern=[[-1, P]], channel_multiplier=1).then_inc(ident_ok, 1)
            pool.memset(expo[:, :], -0.5)
            pool.memset(eps[:, :], EPS).then_inc(ident_zero, 1)
            pool.wait_ge(ident_zero, 2)

            def inverse_root(b, seen, step, done):
                wait(pool, seen, b + 1)
                pool.tensor_tensor(rstd[:, :], mean_var[:, :, 1], eps[:, :], ALU.add).then_inc(step, 1)
                wait(pool, step, b + 1)
                pool.tensor_tensor(rstd[:, :], rstd[:, :], expo[:, :], ALU.pow).then_inc(done, 1)

            def add_bias(b, bias, done):
                r = resid[:, one(b), :, :].rearrange("p b t d -> p (b t) d")
                pool.tensor_tensor(r, r, bias, ALU.add).then_inc(done, 1)

            def split_qk(b, n):
                hi, lo = ((q_hi, q_lo), (k_hi, k_lo))[n % 2]
                wait(pool, qk_ok, 4 * b + n + 1)
                pool.tensor_tensor(lo[:, :], lo[:, :], hi[:, :].bitcast(F32), ALU.subtract).then_inc(qk_lo_ok, 1)

            def add_bo(b):
                add_bias(b, bo_eff[:, one(b), :].to_broadcast([P, T, D]), resid_ok)

            def add_b2(b):
                add_bias(b, b2_bc[:, None, :].to_broadcast([P, T, D]), resid2_ok)

            pool.memset(k_stack[64:96, :, :, :].bitcast(F32), 1.0).then_inc(ident_zero, 1)
            pool.memset(q_stack[64:65, :, :, :].bitcast(F32), 0.0)
            pool.wait_ge(ident_zero, 3)
            pool.memset(k_stack[64:65, :, :, :].bitcast(F32), 0.0).then_inc(consts_ok, 1)
            pool.wait_ge(consts_ok, 1)
            inverse_root(0, stats_ok, var_eps_ok, rstd_ok)
            split_qk(0, 0)
            split_qk(0, 1)
            pool.wait_ge(mlp_hi_ok, 2)
            pool.tensor_tensor(w1_lo[:, :, :], w1_raw, w1_hi[:, :, :].bitcast(F32), ALU.subtract).then_inc(mlp_lo_ok, 1)
            pool.tensor_tensor(w2_lo[:, :, :], w2_raw, w2_hi[:, :, :].bitcast(F32), ALU.subtract).then_inc(mlp_lo_ok, 1)

            def batch(i):
                if live(i + 1, B):
                    inverse_root(i + 1, stats_ok, var_eps_ok, rstd_ok)
                elif live(i, B):
                    wait(pool, xhat_ok, B)
                if live(i, B):
                    split_qk(i, 2)
                    split_qk(i, 3)
                    if isinstance(i, int) and i == 0:
                        wait(pool, u_ok, B + 1)
                    add_bo(i)
                if live(i + 1, B):
                    split_qk(i + 1, 0)
                    split_qk(i + 1, 1)

            over_batches(pool, batch)

            inverse_root(0, stats2_ok, var_eps2_ok, rstd2_ok)
            pool.wait_ge(bc_in, 32)

            def mlp(j, _):
                if live(j, B):
                    for f in range(FT):
                        n = FT * j + f
                        if f == 1 and live(j + 1, B):
                            inverse_root(j + 1, stats2_ok, var_eps2_ok, rstd2_ok)
                            add_b2(j)
                        elif f == 1:
                            add_b2(j)
                        wait(pool, h_ok, n + 1)
                        wait(pool, w2_mm, n - HB + 1)
                        pool.tensor_tensor(h_lo[:, f % HB, :], h_full[:, f % HB, :],
                                           h_hi[:, f % HB, :].bitcast(F32), ALU.subtract).then_inc(h_lo_ok, 1)

            over_mlp_batches(pool, mlp)

        @block.scalar
        def _(act):
            for n, w in enumerate((wt_attn, wt_ffn)):
                act.dma_start(wt_raw[:, n, :, :], w.rearrange("(c p) f -> p c f", p=P)).then_inc(wt_in, 16)
            act.dma_start(bo_bc, bo.rearrange("(a d) -> a d", a=1).to_broadcast([P, D])).then_inc(bc_in, 16)
            act.dma_start(b2_bc[:, :], b2.rearrange("(a d) -> a d", a=1).to_broadcast([P, D])).then_inc(bc_in, 16)
            act.dma_start(w1_raw, w1.rearrange("(c p) f -> p c f", p=P)).then_inc(mlp_in, 16)
            act.dma_start(w2_raw, w2.rearrange("(f p) d -> p f d", p=P)).then_inc(mlp_in, 16)

            def take_x(b, c):
                wait(act, x_turned, 2 * b + c + 1)
                wait(act, gain_ok, b + 1)
                act.activation(xm_hi[:, c, :], work[:, :], ACT.Identity,
                               scale=gain_now[:, 0, c:c + 1]).then_inc(xm_hi_ok, 1)

            def take_qk(b, n):
                wait(act, qk_mm, 4 * b + n + 1)
                wait(act, qk_bias_ok, b + 1)
                k = C * (n % 2) + n // 2
                u = UB * b + 2 * (n // 2)
                done = 128 * (u // 2) if isinstance(u, int) else 256 * b + 128 * (n // 2)
                wait(act, stack_in[0], done)
                wait(act, stack_in[1], done)
                act.activation((q_hi, k_hi)[n % 2][:, :], work[:, :], ACT.Identity,
                               bias=qk_bias_now[:, k:k + 1])
                act.activation((q_lo, k_lo)[n % 2][:, :], work[:, :], ACT.Identity,
                               bias=qk_bias_now[:, k:k + 1]).then_inc(qk_ok, 1)

            def take_v(b, half):
                wait(act, v_mm, 2 * b + half + 1)
                wait(act, pv_ok, T * UB * b)
                act.copy(v_ones[:, 2 * half:2 * half + 2, 0:VH * N_HEADS].rearrange(
                    "p t (h w) -> p t h w", w=VH)[:, :, :, 0:HD],
                         work[:, :].rearrange("p (t h d) -> p t h d", t=2, d=HD)).then_inc(v_ok, 1)

            def take_attn(b, half):
                wait(act, attn_turned, 2 * b + half + 1)
                act.copy(at_hi[:, :, :], work[:, :].rearrange("p (c s) -> p c s", c=C)).then_inc(at_hi_ok, 1)

            def take_pv(u):
                wait(act, pv_ok, T * (u + 1))
                wait(act, pv_turned, u)
                act.copy(pv_sb[:, :], pv[:, :]).then_inc(pv_sb_ok, 1)

            def batch(i):
                for g in range(UB):
                    s = UB * i + g
                    for t in range(TILES):
                        kt, h = t // G, t % G
                        if live(s - LAG, UNITS):
                            u = s - LAG
                            wait(act, shifted_ok, TILES * u + t + 1)
                            if h == 0:
                                wait(act, pv_ok, T * u + kt - 1)
                                if isinstance(u, int) and u == 0 and kt < 2:
                                    wait(act, mlp_lo_ok, 2)
                                    wait(act, bias_ok, 3)
                            act.activation(probs[:, kt % 2, h, :], shifted[t % 2][:, :], ACT.Exp,
                                           scale=float(HD) ** -0.5).then_inc(exp_ok, 1)
                        if t == 2 and live(s - 1, UNITS):
                            wait(act, max_turned, s)
                            if live(s - 2, UNITS):
                                wait(act, max_in[g % 2], (16 * (s - 2 + 2 - g % 2)) if isinstance(s, int)
                                     else 64 * i + 16 * (g - g % 2))
                            act.copy(m_hi[:, :], turn[0:TILES, 0:P]).then_inc(m_hi_ok, 1)
                        if t == 3 and live(s - 3, UNITS):
                            take_pv(s - 3)
                        if live(i, B):
                            if (g, t) in ((0, 8), (0, 12)):
                                take_qk(i, 2 + (t == 12))
                            if (g, t) == (2, 3):
                                take_v(i, 0)
                            if (g, t) == (2, 4):
                                take_v(i, 1)
                        if live(i + 1, B):
                            if (g, t) in ((2, 5), (2, 8)):
                                take_x(i + 1, int(t == 8))
                            if (g, t) in ((2, 11), (2, 14)):
                                take_qk(i + 1, int(t == 14))
                        if live(i - 1, B) and (g, t) in ((3, 1), (3, 8)):
                            take_attn(i - 1, int(t == 8))

            for c in range(C):
                take_x(0, c)
            for n, name in enumerate("qkvo"):
                act.wait_ge(raw_in, 16 * (4))
                src, dst = w_raw[:, n, :, :], wqkv[name][0][:, :, :]
                if name in "qk":
                    for c in range(C):
                        for m in range(2):
                            last = act.copy(in_order(dst[:, c, P * m:P * m + P]),
                                            by_head_in_unit(src[:, c, P * m:P * m + P]))
                else:
                    last = act.copy(dst, src)
                last.then_inc(w_hi_ok, 1)
            for n in range(2):
                take_qk(0, n)
            act.wait_ge(mlp_in, 32)
            act.copy(w1_hi[:, :, :], w1_raw).then_inc(mlp_hi_ok, 1)
            act.copy(w2_hi[:, :, :], w2_raw).then_inc(mlp_hi_ok, 1)
            over_batches(act, batch)

            def take_y(j, c, par):
                wait(act, x2_turned, 2 * j + c + 1)
                wait(act, gain2_ok, j + 1)
                act.activation(ym[par][0][:, c, :], (turn, work)[c][:, :], ACT.Identity,
                               scale=gain_now[:, 1, c:c + 1]).then_inc(ym_hi_ok, 1)

            take_y(0, 0, 0)
            take_y(0, 1, 0)

            def store(b):
                wait(act, y_ok, 2 * b + 2)
                act.dma_start(out_v[:, one(b), :], resid[:, one(b), :, :].rearrange(
                    "p b t d -> p b (t d)")).then_inc(stored, 16)

            def mlp(j, par):
                if live(j, B):
                    for f in range(FT):
                        n = FT * j + f
                        wait(act, w1_mm, n + 1)
                        if f == 0:
                            wait(act, b1_ok, j + 1)
                        wait(act, w2_mm, n - HB + 1)
                        act.activation(h_hi[:, f % HB, :], scores[f % 2][:, :], ACT.Gelu,
                                       bias=b1_now[:, par, f:f + 1]).then_inc(h_hi_ok, 1)
                        wait(act, h_lo_ok, n - HB + 1)
                        act.activation(h_full[:, f % HB, :], scores[f % 2][:, :], ACT.Gelu,
                                       bias=b1_now[:, par, f:f + 1]).then_inc(h_ok, 1)
                        if f in (3, 5) and live(j + 1, B):
                            take_y(j + 1, int(f == 5), 1 - par)
                        if f == 4 and live(j - 1, B):
                            store(j - 1)
                elif live(j - 1, B):
                    store(j - 1)

            over_mlp_batches(act, mlp)
            act.wait_ge(stored, 16 * B)

        @block.vector
        def _(dve):
            def take_stats(b, bn, done, columns):
                for t in range(T):
                    last = dve.bn_stats(stats[:, t, :], resid[:, one(b), t, :].rearrange("p b d -> p (b d)"))
                last.then_inc(bn, 1)
                wait(dve, bn, b + 1)
                columns(b)
                for t in range(T):
                    last = dve.bn_aggr(mean_var[:, t, :], stats[:, t, :])
                last.then_inc(done, 1)

            def normalise(b, root, turned, done):
                wait(dve, root, b + 1)
                wait(dve, turned, 2 * b)
                for t in range(T):
                    last = dve.tensor_scalar(xhat[:, t, :], resid[:, one(b), t, :].rearrange("p b d -> p (b d)"),
                                             mean_var[:, t, 0:1], rstd[:, t:t + 1], ALU.subtract, ALU.mult)
                last.then_inc(done, 1)

            def columns(b):
                wait(dve, xm_lo_ok, 2 * b)
                wait(dve, xm_hi_ok, 2 * b)
                dve.tensor_copy(gain_now[:, 0, :, None], gain[:, 0, :, one(b)]).then_inc(gain_ok, 1)

            def bias_columns(b):
                wait(dve, qk_ok, 4 * b)
                dve.tensor_copy(qk_bias_now[:, :, None], qk_bias[:, :, one(b)]).then_inc(qk_bias_ok, 1)

            def take_x(b, c):
                wait(dve, xm_hi_ok, 2 * b + c + 1)
                dve.scalar_tensor_tensor(xm_lo[:, c, :], work[:, :], gain_now[:, 0, c:c + 1],
                                         xm_hi[:, c, :].bitcast(F32), ALU.mult, ALU.subtract).then_inc(xm_lo_ok, 1)

            def take_attn(b, half):
                wait(dve, at_hi_ok, 2 * b + half + 1)
                dve.tensor_tensor(at_lo[:, :, :], work[:, :].rearrange("p (c s) -> p c s", c=C),
                                  at_hi[:, :, :].bitcast(F32), ALU.subtract).then_inc(at_lo_ok, 1)

            def take_x1(b, half):
                wait(dve, wo_mm, 2 * b + half + 1)
                wait(dve, resid_ok, b + 1)
                r = resid[:, one(b), 2 * half:2 * half + 2, :].rearrange("p b t d -> p (b t) d")
                dve.tensor_tensor(r, work[:, :].rearrange("p (t d) -> p t d", t=2), r, ALU.add).then_inc(x1_ok, 1)

            def take_max(u):
                wait(dve, m_hi_ok, u + 1)
                dve.tensor_tensor(m_lo[:, :], turn[0:TILES, 0:P], m_hi[:, :].bitcast(F32),
                                  ALU.subtract).then_inc(m_lo_ok, 1)

            def take_pv(u, unit, b):
                wait(dve, pv_turned, u + 1)
                tile = turn[:, :].rearrange("p (t h w) -> p t h w", t=T, w=VW)
                dve.reciprocal(recip[:, :, :], tile[:, :, :, HD]).then_inc(recip_ok, 1)
                wait(dve, recip_ok, u + 1)
                if unit == 0:
                    wait(dve, attn_turned, 2 * b)
                dve.tensor_tensor(attn[:, :, unit * G * HD:(unit + 1) * G * HD].rearrange(
                    "p t (h d) -> p t h d", d=HD), tile[:, :, :, 0:HD],
                    recip[:, :, :, None].to_broadcast([P, T, G, HD]), ALU.mult).then_inc(attn_ok, 1)

            dve.wait_ge(x_in[0], 16)
            take_stats(0, bn_ok, stats_ok, lambda b: None)
            normalise(0, rstd_ok, x_turned, xhat_ok)
            dve.wait_ge(qk_rows_in, 32)
            dve.tensor_copy(in_order(qk_rows_p), by_head_in_unit(qk_rows)).then_inc(rows_perm, 1)
            dve.wait_ge(rows_turned, 1)
            dve.tensor_copy(vec_cols[:, :], turn[:, 0:n_vec + 2 * C]).then_inc(cols_ok, 1)
            dve.tensor_copy(cond_cols[:, :, :].rearrange("p c b -> p (c b)"), turn[:, 64:64 + C * B]).then_inc(cols_ok, 1)
            dve.wait_ge(mod_mm, 1)
            dve.wait_ge(cols_ok, 2)
            dve.tensor_tensor(mod[:, :, :, :].rearrange("p n c b -> p (n c) b"),
                              scores[0][:, 0:4 * C * B].rearrange("p (n b) -> p n b", b=B),
                              vec_cols[:, at["bt_attn"]:at["bt_attn"] + 4 * C, None].to_broadcast([P, 4 * C, B]),
                              ALU.add).then_inc(mod_step, 1)
            dve.wait_ge(mod_step, 1)
            dve.tensor_scalar(mod[:, :, C:2 * C, :], mod[:, :, C:2 * C, :], 1.0, None, ALU.add).then_inc(mod_step, 1)
            dve.wait_ge(mod_step, 2)
            for n, (w, b) in enumerate((("ln1_w", "ln1_b"), ("ln2_w", "ln2_b"))):
                dve.tensor_tensor(gain[:, n, :, :], mod[:, n, C:2 * C, :],
                                  vec_cols[:, at[w]:at[w] + C, None].to_broadcast([P, C, B]),
                                  ALU.mult).then_inc(mod_step, 1)
            for n, (w, b) in enumerate((("ln1_w", "ln1_b"), ("ln2_w", "ln2_b"))):
                dve.tensor_tensor(offs[:, n, :, :], mod[:, n, C:2 * C, :],
                                  vec_cols[:, at[b]:at[b] + C, None].to_broadcast([P, C, B]),
                                  ALU.mult).then_inc(mod_step, 1)
            dve.wait_ge(mod_step, 6)
            dve.tensor_tensor(offs[:, :, :, :], offs[:, :, :, :], mod[:, :, 0:C, :], ALU.add).then_inc(mod_step, 1)
            dve.wait_ge(mod_step, 7)
            dve.tensor_copy(offs_hi[:, :, :], offs[:, 0, :, :]).then_inc(mod_step, 1)
            dve.wait_ge(mod_step, 8)
            dve.tensor_tensor(offs_lo[:, :, :], offs[:, 0, :, :], offs_hi[:, :, :].bitcast(F32),
                              ALU.subtract).then_inc(mod_step, 1)
            columns(0)
            for c in range(C):
                take_x(0, c)
            for n, name in enumerate("qkvo"):
                dve.wait_ge(w_hi_ok, n + 1)
                src, hi, lo = w_raw[:, n, :, :], wqkv[name][0][:, :, :].bitcast(F32), wqkv[name][1][:, :, :]
                if name in "qk":
                    for c in range(C):
                        for m in range(2):
                            k = slice(P * m, P * m + P)
                            last = dve.tensor_tensor(in_order(lo[:, c, k]), by_head_in_unit(src[:, c, k]),
                                                     in_order(hi[:, c, k]), ALU.subtract)
                else:
                    last = dve.tensor_tensor(lo, src, hi, ALU.subtract)
                last.then_inc(w_lo_ok, 1)
            dve.wait_ge(bias_mm, 1)
            dve.tensor_tensor(qk_bias[:, :, :], scores[1][:, 0:2 * C * B].rearrange("p (n b) -> p n b", b=B),
                              vec_cols[:, n_vec:n_vec + 2 * C, None].to_broadcast([P, 2 * C, B]),
                              ALU.add).then_inc(bias_ok, 1)
            dve.tensor_tensor(v_bias[:, :, :], scores[1][:, 2 * C * B:3 * C * B].rearrange("p (n b) -> p n b", b=B),
                              vec_cols[:, at["bv"]:at["bv"] + C, None].to_broadcast([P, C, B]),
                              ALU.add).then_inc(u_ok, 1)
            dve.wait_ge(bias_ok, 1)
            bias_columns(0)
            dve.memset(v_ones[:, :, :], 1.0).then_inc(bias_ok, 1)
            dve.wait_ge(bc_in, 32)
            for b in range(B):
                dve.wait_ge(u_mm, b + 1)
                dve.tensor_tensor(bo_eff[:, b, :], shifted[b % 2][:, 0:D], bo_bc, ALU.add).then_inc(u_ok, 1)
            dve.wait_ge(bias_mm, 2)
            dve.tensor_tensor(b1_eff[:, :, :], pv[:, 0:FT * B].rearrange("p (n b) -> p n b", b=B),
                              vec_cols[:, at["b1"]:at["b1"] + FT, None].to_broadcast([P, FT, B]),
                              ALU.add).then_inc(bias_ok, 1)

            def batch(i):
                for g in range(UB):
                    s = UB * i + g
                    for t in range(TILES):
                        if live(s, UNITS):
                            wait(dve, scores_ok, TILES * s + t + 1)
                            if t == 0:
                                wait(dve, max_turned, s - 1)
                            dve.tensor_reduce(neg_max[:, g % 2, t:t + 1], scores[(TILES * g + t) % 3][:, :], AX.X, ALU.max,
                                              negate=True).then_inc(max_ok, 1)
                        if t == 4 and live(s - 1, UNITS):
                            take_max(s - 1)
                        if t == TV + 1 and live(s - 3, UNITS):
                            take_pv(s - 3, (g + 1) % UB, i if g == 3 else i - 1)
                        if live(i + 1, B):
                            if (g, t) == (0, 5):
                                wait(dve, x_in[1], 16)
                                if not isinstance(i, int) or i > 0:
                                    wait(dve, x_in[2], 16)
                                take_stats(i + 1, bn_ok, stats_ok, columns)
                            if (g, t) == (1, 2):
                                normalise(i + 1, rstd_ok, x_turned, xhat_ok)
                            if (g, t) == (1, 4):
                                bias_columns(i + 1)
                            if (g, t) in ((2, 6), (2, 9)):
                                take_x(i + 1, int(t == 9))
                        if live(i - 1, B):
                            if (g, t) in ((3, 2), (3, 9)):
                                take_attn(i - 1, int(t == 9))
                            if (g, t) in ((3, 6), (3, 13)):
                                take_x1(i - 1, int(t == 13))

            over_batches(dve, batch)

            def columns2(j, par):
                wait(dve, ym_lo_ok, 2 * j)
                wait(dve, ym_hi_ok, 2 * j)
                dve.tensor_copy(gain_now[:, 1, :, None], gain[:, 1, :, one(j)]).then_inc(gain2_ok, 1)
                wait(dve, h_ok, FT * (j - 1))
                dve.tensor_copy(b1_now[:, par, :, None], b1_eff[:, :, one(j)]).then_inc(b1_ok, 1)

            def take_y(j, c, par):
                wait(dve, ym_hi_ok, 2 * j + c + 1)
                dve.scalar_tensor_tensor(ym[par][1][:, c, :], (turn, work)[c][:, :], gain_now[:, 1, c:c + 1],
                                         ym[par][0][:, c, :].bitcast(F32), ALU.mult,
                                         ALU.subtract).then_inc(ym_lo_ok, 1)

            wait(dve, x1_ok, 2)
            take_stats(0, bn2_ok, stats2_ok, lambda b: columns2(b, 0))
            normalise(0, rstd2_ok, x2_turned, xhat2_ok)
            take_y(0, 0, 0)
            take_y(0, 1, 0)

            def mlp(j, par):
                if live(j + 1, B):
                    wait(dve, x1_ok, 2 * j + 4)
                    take_stats(j + 1, bn2_ok, stats2_ok, lambda b: columns2(b, 1 - par))
                    normalise(j + 1, rstd2_ok, x2_turned, xhat2_ok)
                if live(j - 1, B):
                    wait(dve, w2_mm, FT * j)
                    wait(dve, resid2_ok, j)
                    for half in range(2):
                        r = resid[:, one(j - 1), 2 * half:2 * half + 2, :].rearrange("p b t d -> p (b t) d")
                        dve.tensor_tensor(r, sums[1 - par][half][:, :].rearrange("p (t d) -> p t d", t=2), r,
                                          ALU.add).then_inc(y_ok, 1)
                if live(j + 1, B):
                    for c in range(C):
                        take_y(j + 1, c, 1 - par)

            over_mlp_batches(dve, mlp)

        @block.tensor
        def _(pe):
            TERMS = ((0, 0), (0, 1), (1, 0))

            def product(dst, lhs, rhs):
                n = len(lhs) * len(TERMS)
                k = 0
                for left, right in zip(lhs, rhs):
                    for a, b in TERMS:
                        last = pe.matmul(dst, left[a], right[b], start=(k == 0), stop=(k == n - 1))
                        k += 1
                return last

            def parts(pair, *index):
                return [p[index] for p in pair]

            ALL = slice(None)
            xm, am = (xm_hi, xm_lo), (at_hi, at_lo)

            def turn_x(b, c):
                wait(pe, xhat_ok, b + 1)
                for t in range(T):
                    last = pe.transpose(work[:, P * t:P * t + P], xhat[:, t, P * c:P * c + P], ident[:, :])
                last.then_inc(x_turned, 1)

            def project_qk(b, n):
                w = wqkv["qk"[n % 2]]
                m = n // 2
                product(work[:, :], [parts(w, ALL, c, slice(P * m, P * m + P)) for c in range(C)],
                        [parts(xm, ALL, c, ALL) for c in range(C)]).then_inc(qk_mm, 1)

            def project_v(b, half):
                for t in range(2):
                    k = P * (2 * half + t)
                    last = product(work[:, D * t:D * t + D], [parts(xm, ALL, c, slice(k, k + P)) for c in range(C)],
                                   [parts(wqkv["v"], ALL, c, ALL) for c in range(C)])
                last.then_inc(v_mm, 1)

            def turn_attn(b, half):
                wait(pe, attn_ok, UB * (b + 1))
                for c in range(C):
                    for t in range(2):
                        k = P * (2 * c + t)
                        last = pe.transpose(work[:, k:k + P], attn[:, 2 * half + t, P * c:P * c + P], ident[:, :])
                last.then_inc(attn_turned, 1)

            def project_out(b, half):
                for t in range(2):
                    k = P * t
                    last = product(work[:, D * t:D * t + D], [parts(am, ALL, c, slice(k, k + P)) for c in range(C)],
                                   [parts(wqkv["o"], ALL, c, ALL) for c in range(C)])
                last.then_inc(wo_mm, 1)

            def turn_max(u, slot):
                wait(pe, max_ok, TILES * (u + 1))
                wait(pe, attn_ok, u - 2)
                pe.transpose(turn[0:TILES, 0:P], neg_max[:, slot, :], ident[:, :]).then_inc(max_turned, 1)

            def turn_pv(u):
                wait(pe, pv_sb_ok, u + 1)
                if live(u + LAG, UNITS):
                    wait(pe, m_lo_ok, u + LAG + 1)
                else:
                    wait(pe, attn_ok, u)
                for t in range(T):
                    last = pe.transpose(turn[:, P * t:P * t + P], pv_sb[:, P * t:P * t + P], ident[:, :])
                last.then_inc(pv_turned, 1)

            def sum_values(u, unit, kt):
                wait(pe, exp_ok, TILES * u + G * kt + G)
                if kt == 0:
                    wait(pe, pv_sb_ok, u)
                for h in range(G):
                    last = pe.matmul(pv[VW * h:VW * h + VW, :], v_ones[:, kt, VH * (G * unit + h):VH * (G * unit + h) + VW],
                                     probs[:, kt % 2, h, :], start=(kt == 0), stop=(kt == T - 1))
                last.then_inc(pv_ok, 1)

            def batch(i):
                for g in range(UB):
                    s = UB * i + g
                    for t in range(TILES):
                        if live(s, UNITS):
                            if t == 0:
                                wait(pe, stack_in[g % 2], 128 * (s // 2 + 1) if isinstance(s, int)
                                     else 256 * i + 128 * (g // 2 + 1))
                            n = TILES * g + t
                            wait(pe, max_ok, TILES * UB * i + n + 1 - (1 if n == 0 else 4 if n < 3 else 3))
                            h, qt = t // T, t % T
                            pe.matmul(scores[n % 3][:, :], q_stack[0:K_A, g, h, P * qt:P * qt + P],
                                      k_stack[0:K_A, g, h, :], start=True, stop=True).then_inc(scores_ok, 1)
                        if live(s - LAG, UNITS):
                            u, slot = s - LAG, (g + LAG) % UB
                            if t == 0:
                                wait(pe, max_in[slot % 2], 32 * (u // 2 + 1) if isinstance(u, int)
                                     else 64 * i + 32 * (g // 2))
                            wait(pe, exp_ok, TILES * u + t - 1)
                            kt, h = t // G, t % G
                            pe.matmul(shifted[t % 2][:, :], k_stack[0:K_B, slot, h, P * kt:P * kt + P],
                                      q_stack[0:K_B, slot, h, :], start=True, stop=True).then_inc(shifted_ok, 1)
                            if t in (6, 10, 14):
                                if t == 6 and slot == 0:
                                    wait(pe, v_ok, 2 * i + 2)
                                sum_values(u, slot, (t - 6) // G)
                        if t == 2 and live(s - 3, UNITS):
                            sum_values(s - 3, (g + 1) % UB, T - 1)
                        if t == 2 and live(s - 1, UNITS):
                            turn_max(s - 1, (g + 1) % 2)
                        if t == TV and live(s - 3, UNITS):
                            turn_pv(s - 3)
                        if live(i, B):
                            if (g, t) == (0, 8):
                                wait(pe, qk_ok, 4 * i + 2)
                                project_qk(i, 2)
                            if (g, t) == (0, 12):
                                wait(pe, qk_ok, 4 * i + 3)
                                project_qk(i, 3)
                            if (g, t) == (1, 12):
                                wait(pe, qk_ok, 4 * i + 4)
                                project_v(i, 0)
                            if (g, t) == (2, 3):
                                wait(pe, v_ok, 2 * i + 1)
                                project_v(i, 1)
                        if live(i + 1, B):
                            if (g, t) == (2, 5):
                                wait(pe, v_ok, 2 * i + 2)
                                turn_x(i + 1, 0)
                            if (g, t) == (2, 8):
                                wait(pe, xm_lo_ok, 2 * i + 3)
                                turn_x(i + 1, 1)
                            if (g, t) == (2, 11):
                                wait(pe, xm_lo_ok, 2 * i + 4)
                                project_qk(i + 1, 0)
                            if (g, t) == (2, 14):
                                wait(pe, qk_ok, 4 * i + 5)
                                project_qk(i + 1, 1)
                        if live(i - 1, B):
                            if (g, t) == (3, 1):
                                if live(i + 1, B):
                                    wait(pe, qk_ok, 4 * i + 6)
                                else:
                                    wait(pe, v_ok, 2 * B)
                                turn_attn(i - 1, 0)
                            if (g, t) == (3, 5):
                                wait(pe, at_lo_ok, 2 * i - 1)
                                project_out(i - 1, 0)
                            if (g, t) == (3, 8):
                                wait(pe, x1_ok, 2 * i - 1)
                                turn_attn(i - 1, 1)
                            if (g, t) == (3, 12):
                                wait(pe, at_lo_ok, 2 * i)
                                project_out(i - 1, 1)
                            if (g, t) == (3, TILES - 1):
                                wait(pe, x1_ok, 2 * i)
            pe.wait_ge(ident_ok, 1)
            pe.wait_ge(cond_in, 16)
            pe.wait_ge(vec_in, 16 * len(vectors))
            pe.wait_ge(rows_perm, 1)
            pe.transpose(turn[:, 0:n_vec], vec_rows, ident[0:n_vec, 0:n_vec])
            pe.transpose(turn[:, n_vec:n_vec + 2 * C], qk_rows_p, ident[0:2 * C, 0:2 * C])
            for c in range(C):
                last = pe.transpose(turn[:, 64 + B * c:64 + B * c + B], attn[0:B, 3, P * c:P * c + P],
                                    ident[0:B, 0:B])
            last.then_inc(rows_turned, 1)
            pe.wait_ge(cols_ok, 2)
            pe.wait_ge(wt_in, 32)
            for n in range(2):
                for m in range(2 * C):
                    for c in range(C):
                        k = B * (2 * C * n + m)
                        last = pe.matmul(scores[0][:, k:k + B], wt_raw[:, n, c, P * m:P * m + P], cond_cols[:, c, :],
                                         start=(c == 0), stop=(c == C - 1))
            last.then_inc(mod_mm, 1)
            turn_x(0, 0)
            pe.wait_ge(xm_lo_ok, 1)
            turn_x(0, 1)
            pe.wait_ge(mod_step, 9)
            pe.wait_ge(w_lo_ok, 2)
            for n in range(2):
                for m in range(C):
                    k = B * (C * n + m)
                    product(scores[1][:, k:k + B], [parts(wqkv["qk"[n]], ALL, c, slice(P * m, P * m + P))
                                                    for c in range(C)],
                            [parts((offs_hi, offs_lo), ALL, c, ALL) for c in range(C)])
            for m in range(C):
                for c in range(C):
                    k = B * (2 * C + m)
                    last = pe.matmul(scores[1][:, k:k + B], w_raw[:, 2, c, P * m:P * m + P], offs[:, 0, c, :],
                                     start=(c == 0), stop=(c == C - 1))
            last.then_inc(bias_mm, 1)
            pe.wait_ge(xm_lo_ok, 2)
            project_qk(0, 0)
            pe.wait_ge(qk_ok, 1)
            project_qk(0, 1)
            for b in range(B):
                wait(pe, u_ok, max(1, b))
                for c in range(C):
                    last = pe.matmul(shifted[b % 2][:, 0:D], v_bias[:, c, b:b + 1].to_broadcast([P, P]),
                                     w_raw[:, 3, c, :], start=(c == 0), stop=(c == C - 1))
                last.then_inc(u_mm, 1)
            pe.wait_ge(mlp_in, 32)
            for m in range(FT):
                for c in range(C):
                    last = pe.matmul(pv[:, B * m:B * m + B], w1_raw[:, c, P * m:P * m + P], offs[:, 1, c, :],
                                     start=(c == 0), stop=(c == C - 1))
            last.then_inc(bias_mm, 1)
            pe.wait_ge(bias_ok, 3)
            pe.wait_ge(u_ok, B + 1)
            pe.wait_ge(w_lo_ok, 4)
            over_batches(pe, batch)

            def turn_y(j, c):
                wait(pe, xhat2_ok, j + 1)
                wait(pe, ym_lo_ok, 2 * j - 1 + c)
                for t in range(T):
                    last = pe.transpose((turn, work)[c][:, P * t:P * t + P], xhat[:, t, P * c:P * c + P],
                                        ident[:, :])
                last.then_inc(x2_turned, 1)

            turn_y(0, 0)
            turn_y(0, 1)
            pe.wait_ge(mlp_lo_ok, 2)

            def down(j, par, f):
                wait(pe, h_lo_ok, FT * j + f + 1)
                for t in range(T):
                    acc = sums[par][t // 2][:, D * (t % 2):D * (t % 2) + D]
                    for n, (a, b) in enumerate(TERMS):
                        last = pe.matmul(acc, (h_hi, h_lo)[a][:, f % HB, P * t:P * t + P], (w2_hi, w2_lo)[b][:, f, :],
                                         start=(f == 0 and n == 0 and t % 2 == 0), stop=(f == FT - 1 and n == 2),
                                         skip_group_check=True)
                last.then_inc(w2_mm, 1)

            def mlp(j, par):
                for f in range(FT):
                    n = FT * j + f
                    if live(j, B):
                        if f == 0:
                            wait(pe, ym_lo_ok, 2 * j + 2)
                        wait(pe, h_ok, n - 1)
                        product(scores[f % 2][:, :], [parts((w1_hi, w1_lo), ALL, c, slice(P * f, P * f + P))
                                                      for c in range(C)],
                                [[y[:, c, :] for y in ym[par]] for c in range(C)]).then_inc(w1_mm, 1)
                    if f >= 2 and live(j, B):
                        down(j, par, f - 2)
                    if f < 2 and live(j - 1, B):
                        down(j - 1, 1 - par, FT - 2 + f)
                    if f in (3, 5) and live(j + 1, B):
                        turn_y(j + 1, int(f == 5))
                    if f == FT - 1 and live(j - 1, B):
                        wait(pe, y_ok, 2 * j)

            over_mlp_batches(pe, mlp)


_PRE = "L0_cond_"
_INS = ["x", "cond_1024"] + [_PRE + n for n in (
    "ln1_w", "ln1_b", "ln2_w", "ln2_b", "wq", "bq", "wk", "bk", "wv", "bv", "wo", "bo",
    "wt_attn", "bt_attn", "wt_ffn", "bt_ffn", "w1", "b1", "w2", "b2")]


def kernel(**inputs):
    import numpy as _np
    import concourse.bacc as _bacc
    from concourse import mybir as _mybir
    from concourse.bass_utils import run_bass_kernel_spmd as _run

    nc = _bacc.Bacc("TRN2", target_bir_lowering=False, num_devices=1)
    arrays, args = {}, []
    for name in _INS:
        a = _np.ascontiguousarray(inputs[name])
        arrays[f"in_{name}_dram"] = a
        args.append(nc.dram_tensor(f"in_{name}_dram", a.shape, _mybir.dt.from_np(a.dtype), kind="ExternalInput").ap())
    shape = inputs["x"].shape
    args.append(nc.dram_tensor("out_0_dram", shape, _mybir.dt.float32, kind="ExternalOutput").ap())
    cond_transformer_block(nc, *args)
    r = _run(nc, [arrays], core_ids=[0])
    return r.results[0]["out_0_dram"]
```

```python
from contextlib import ExitStack

import concourse.bass as bass
from concourse import mybir

F32 = mybir.dt.float32
F32R = mybir.dt.float32r
ALU = mybir.AluOpType
ACT = mybir.ActivationFunctionType
AX = mybir.AxisListType

P = 128
N_HEADS = 16
EPS = 1e-5


def cond_transformer_block(nc, x, cond, ln1_w, ln1_b, ln2_w, ln2_b, wq, bq, wk, bk, wv, bv, wo, bo,
                           wt_attn, bt_attn, wt_ffn, bt_ffn, w1, b1, w2, b2, out):
    B, S, D = x.shape
    F = w1.shape[1]
    HD = D // N_HEADS
    T = S // P
    C = D // P
    FT = F // P
    G = 4
    UB = N_HEADS // G
    UNITS = B * UB
    TILES = G * T
    LAG = 2
    K_A = 4 * HD + 1
    K_B = K_A + 2
    VH = HD + 1
    VW = 32
    TV = 12
    HB = 4
    assert S == 512 and D == 256 and HD == 16 and F == 1024

    with ExitStack() as ctx:
        def sb(name, shape, dt=F32):
            return ctx.enter_context(nc.sbuf_tensor(name, shape, dt))

        def sem(name):
            return ctx.enter_context(nc.semaphore(name))

        resid = sb("resid", [P, B, T, D])
        wqkv = {}
        for n in ("q", "k", "v", "o"):
            wqkv[n] = (sb(f"w{n}_hi", [P, C, D], F32R), sb(f"w{n}_lo", [P, C, D], F32R))
        w1_hi, w1_lo = sb("w1_hi", [P, C, F], F32R), sb("w1_lo", [P, C, F], F32R)
        w2_hi, w2_lo = sb("w2_hi", [P, FT, D], F32R), sb("w2_lo", [P, FT, D], F32R)
        q_stack = sb("q_stack", [P, UB, G, S], F32R)
        k_stack = sb("k_stack", [P, UB, G, S], F32R)
        probs = sb("probs", [P, 2, G, S])
        v_ones = sb("v_ones", [P, T, VH * N_HEADS + VW - VH])
        with nc.sbuf_tensor("xhat", [P, T, D], F32) as xhat:
            pass
        at_hi, at_lo = sb("at_hi", [P, C, S // 2], F32R), sb("at_lo", [P, C, S // 2], F32R)
        xm_hi, xm_lo = sb("xm_hi", [P, C, S], F32R), sb("xm_lo", [P, C, S], F32R)
        q_hi, q_lo = sb("q_hi", [P, S], F32R), sb("q_lo", [P, S])
        k_hi, k_lo = sb("k_hi", [P, S], F32R), sb("k_lo", [P, S])
        pv_sb = sb("pv_sb", [P, S])
        attn = sb("attn", [P, T, D])
        v_next = sb("v_next", [P, T, D])
        bo_eff = sb("bo_eff", [P, B, D])
        b2_bc = sb("b2_bc", [P, D])
        ident = sb("ident", [P, P])
        neg_max = sb("neg_max", [P, 2, TILES])
        m_hi, m_lo = sb("m_hi", [TILES, P], F32R), sb("m_lo", [TILES, P], F32R)
        recip = sb("recip", [P, T, G])
        stats = sb("stats", [P, T, 6])
        mean_var = sb("mean_var", [P, T, 2])
        rstd, eps, expo = sb("rstd", [P, T]), sb("eps", [P, T]), sb("expo", [P, T])
        n_vec = 4 * C + C + 2 * 2 * C + FT
        vec_cols = sb("vec_cols", [P, n_vec + 2 * C])
        cond_cols = sb("cond_cols", [P, C, B])
        mod = sb("mod", [P, 2, 2 * C, B])
        gain = sb("gain", [P, 2, C, B])
        offs = sb("offs", [P, 2, C, B])
        offs_hi, offs_lo = sb("offs_hi", [P, C, B], F32R), sb("offs_lo", [P, C, B], F32R)
        qk_bias = sb("qk_bias", [P, 2 * C, B])
        v_bias = sb("v_bias", [P, C, B])
        b1_eff = sb("b1_eff", [P, FT, B])
        gain_now = sb("gain_now", [P, 2, C])
        qk_bias_now = sb("qk_bias_now", [P, 2 * C])
        b1_now = sb("b1_now", [P, 2, FT])

        w_raw = resid[:, 4:6, :, :].rearrange("p b t d -> p (b t) d").rearrange("p (n c) d -> p n c d", c=C)
        wt_raw = resid[:, 6:8, :, :].rearrange("p b t d -> p b (t d)").rearrange("p n (c f) -> p n c f", c=C)
        vec_rows, qk_rows, qk_rows_p = attn[0:n_vec, 0, 0:P], attn[0:2 * C, 1, 0:P], attn[0:2 * C, 2, 0:P]
        cond_rows = attn[0:B, 3, :]
        bo_bc = pv_sb[:, 0:D]
        probs_flat = probs[:, :, :, :].rearrange("p a g s -> p (a g s)")
        w1_raw = probs_flat[:, 0:C * F].rearrange("p (c f) -> p c f", c=C)
        w2_raw = probs_flat[:, C * F:C * F + FT * D].rearrange("p (f d) -> p f d", f=FT)
        h_full = probs[:, 0, :, :]
        h_hi = q_stack[:, 0, :, :]
        h_lo = q_stack[:, 1, :, :]
        ym = [(xm_hi[:, :, :], xm_lo[:, :, :]), (k_stack[:, 0, 0:C, :], k_stack[:, 1, 0:C, :])]

        VB, MOD = FT * B, FT * B + C * B

        scores = [ctx.enter_context(nc.psum_tensor(f"scores{n}", [P, S], F32)) for n in range(3)]
        shifted = [ctx.enter_context(nc.psum_tensor(f"shifted{n}", [P, S], F32)) for n in range(2)]
        pv = ctx.enter_context(nc.psum_tensor("pv", [P, S], F32))
        turn = ctx.enter_context(nc.psum_tensor("turn", [P, S], F32))
        work = ctx.enter_context(nc.psum_tensor("work", [P, S], F32))

        sums = [shifted, (scores[2], pv)]

        x_in = [sem("x0_in"), sem("x1_in"), sem("x4_in")]
        vec_in, cond_in = sem("vec_in"), sem("cond_in")
        wt_in, raw_in, raw_vo_in = [sem("wt_attn_in"), sem("wt_ffn_in")], sem("raw_qk_in"), sem("raw_vo_in")
        mlp_in, bc_in, qk_rows_in = sem("mlp_in"), sem("bc_in"), sem("qk_rows_in")
        ident_zero, ident_ok, consts_ok = sem("ident_zero"), sem("ident_ok"), sem("consts_ok")
        rows_turned, cols_ok, mod_mm, mod_step = sem("rows_turned"), sem("cols_ok"), sem("mod_mm"), sem("mod_step")
        rows_perm, v_ones_ok = sem("rows_perm"), sem("v_ones_ok")
        bias_mm, bias_ok, u_mm, u_ok = sem("bias_mm"), sem("bias_ok"), sem("u_mm"), sem("u_ok")
        w_hi_ok, w_lo_ok, mlp_hi_ok, mlp_lo_ok = sem("w_hi_ok"), sem("w_lo_ok"), sem("mlp_hi_ok"), sem("mlp_lo_ok")
        stack_in = [sem("stack_even_in"), sem("stack_odd_in")]
        max_in = [sem("max_even_in"), sem("max_odd_in")]
        scores_ok, shifted_ok, pv_ok = sem("scores_ok"), sem("shifted_ok"), sem("pv_ok")
        max_turned, pv_turned = sem("max_turned"), sem("pv_turned")
        qk_mm, v_mm, x_turned, attn_turned, wo_mm = (sem("qk_mm"), sem("v_mm"), sem("x_turned"),
                                                     sem("attn_turned"), sem("wo_mm"))
        max_ok, m_lo_ok, qk_lo_ok, xm_lo_ok = sem("max_ok"), sem("m_lo_ok"), sem("qk_lo_ok"), sem("xm_lo_ok")
        recip_ok, attn_ok, at_lo_ok, x1_ok = sem("recip_ok"), sem("attn_ok"), sem("at_lo_ok"), sem("x1_ok")
        bn_ok, stats_ok, xhat_ok = sem("bn_ok"), sem("stats_ok"), sem("xhat_ok")
        gain_ok, qk_bias_ok, gain2_ok, b1_ok = sem("gain_ok"), sem("qk_bias_ok"), sem("gain2_ok"), sem("b1_ok")
        exp_ok, m_hi_ok, qk_ok, xm_hi_ok = sem("exp_ok"), sem("m_hi_ok"), sem("qk_ok"), sem("xm_hi_ok")
        pv_sb_ok, at_hi_ok, v_next_ok = sem("pv_sb_ok"), sem("at_hi_ok"), sem("v_next_ok")
        var_eps_ok, rstd_ok, resid_ok, v_ok = sem("var_eps_ok"), sem("rstd_ok"), sem("resid_ok"), sem("v_ok")
        bn2_ok, stats2_ok, xhat2_ok = sem("bn2_ok"), sem("stats2_ok"), sem("xhat2_ok")
        var_eps2_ok, rstd2_ok = sem("var_eps2_ok"), sem("rstd2_ok")
        resid2_ok, x2_turned, ym_hi_ok, ym_lo_ok = (sem("resid2_ok"), sem("x2_turned"), sem("ym_hi_ok"),
                                                    sem("ym_lo_ok"))
        w1_mm, h_hi_ok, h_ok, h_lo_ok, w2_mm, y_ok, stored = (sem("w1_mm"), sem("h_hi_ok"), sem("h_ok"),
                                                              sem("h_lo_ok"), sem("w2_mm"), sem("y_ok"),
                                                              sem("stored"))

        x_v = x.rearrange("b (p t) d -> p b (t d)", t=T)
        out_v = out.rearrange("b (p t) d -> p b (t d)", t=T)

        def live(n, end):
            return not isinstance(n, int) or 0 <= n < end

        def wait(eng, s, value):
            if not isinstance(value, int) or value > 0:
                eng.wait_ge(s, value)

        def over_batches(eng, body):
            body(0)
            with eng.Fori(1, B - 1) as i:
                body(i)
            body(B - 1)
            body(B)

        def over_mlp_batches(eng, body):
            body(0, 0)
            with eng.Fori(0, B // 2 - 1) as k:
                body(2 * k + 1, 1)
                body(2 * k + 2, 0)
            body(B - 1, 1)
            body(B, 0)

        at = {}
        row = 0
        vectors = [("ln1_w", ln1_w, C), ("ln1_b", ln1_b, C), ("ln2_w", ln2_w, C), ("ln2_b", ln2_b, C),
                   ("bv", bv, C), ("bt_attn", bt_attn, 2 * C), ("bt_ffn", bt_ffn, 2 * C), ("b1", b1, FT)]
        for name, _, n in vectors:
            at[name] = row
            row += n
        assert row == n_vec

        def by_head_in_unit(ap):
            return ap.rearrange("p (u h d) -> p u d h", u=2, h=G)

        def in_order(ap):
            return ap.rearrange("p (u d h) -> p u d h", u=2, h=G)

        block = ctx.enter_context(nc.Block())

        @block.sync
        def _(sp):
            sp.dma_start(resid[:, 0, :, :], x_v[:, 0, :].rearrange("p (t d) -> p t d", t=T)).then_inc(x_in[0], 16)
            sp.dma_start(cond_rows, cond).then_inc(cond_in, 16)
            for name, v, n in vectors:
                sp.dma_start(attn[at[name]:at[name] + n, 0, 0:P],
                             v.rearrange("(n p) -> n p", p=P)).then_inc(vec_in, 16)
            sp.dma_start(attn[0:C, 1, 0:P], bq.rearrange("(n p) -> n p", p=P)).then_inc(qk_rows_in, 16)
            sp.dma_start(attn[C:2 * C, 1, 0:P], bk.rearrange("(n p) -> n p", p=P)).then_inc(qk_rows_in, 16)
            for n, w in ((2, wv), (3, wo)):
                sp.dma_start(w_raw[:, n, :, :], w.rearrange("(c p) f -> p c f", p=P)).then_inc(raw_vo_in, 16)
            sp.dma_start(bo_bc, bo.rearrange("(a d) -> a d", a=1).to_broadcast([P, D])).then_inc(bc_in, 16)
            sp.dma_start(b2_bc[:, :], b2.rearrange("(a d) -> a d", a=1).to_broadcast([P, D])).then_inc(bc_in, 16)
            sp.dma_start(w1_raw, w1.rearrange("(c p) f -> p c f", p=P)).then_inc(mlp_in, 16)
            sp.dma_start(w2_raw, w2.rearrange("(f p) d -> p f d", p=P)).then_inc(mlp_in, 16)
            sp.dma_start(resid[:, 1:4, :, :],
                         x_v[:, 1:4, :].rearrange("p b (t d) -> p b t d", t=T)).then_inc(x_in[1], 16)

            def batch(i):
                for g in range(UB):
                    u = UB * i + g + 1
                    slot, m = (g + 1) % UB, ((g + 1) % UB) // 2
                    if live(u, UNITS):
                        load_stacks(u, slot, i if g + 1 < UB else i + 1, m)
                    if live(u - 2, UNITS):
                        load_max(u - 2, (g - 1) % UB)
                    if isinstance(i, int) and (i, g) == (0, 2):
                        sp.wait_ge(bias_ok, 2)
                        sp.wait_ge(u_ok, B + 1)
                        sp.wait_ge(w_lo_ok, 4)
                        sp.dma_start(resid[:, 4:B, :, :],
                                     x_v[:, 4:B, :].rearrange("p b (t d) -> p b t d", t=T)).then_inc(x_in[2], 16)

            def load_stacks(u, slot, b, m):
                split, freed = 4 * b + 2 * m + 2, TILES * (u - UB + 1)
                if not isinstance(u, int):
                    split, freed = sp.to_reg(split), sp.to_reg(freed)
                wait(sp, qk_lo_ok, split)
                wait(sp, shifted_ok, freed)
                rows = slice(64 * (slot % 2), 64 * (slot % 2) + 64)
                qh, kh = q_hi[:, :].bitcast(F32), k_hi[:, :].bitcast(F32)
                for stack, parts in ((q_stack, (qh, qh, q_lo, q_lo)), (k_stack, (kh, k_lo, kh, k_lo))):
                    for n, part in enumerate(parts):
                        sp.dma_start(stack[HD * n:HD * n + HD, slot, :, :].bitcast(F32),
                                     part[rows, :]).then_inc(stack_in[slot % 2], 16)

            def load_max(u, slot):
                wait(sp, m_lo_ok, u + 1)
                for n, part in enumerate((m_hi, m_lo)):
                    sp.dma_start(q_stack[K_A + n:K_A + n + 1, slot, :, :].bitcast(F32),
                                 part[:, :].bitcast(F32)).then_inc(max_in[slot % 2], 16)

            load_stacks(0, 0, 0, 0)
            over_batches(sp, batch)

        def one(i):
            return slice(i, i + 1) if isinstance(i, int) else bass.ds(i, 1)

        @block.gpsimd
        def _(pool):
            pool.memset(ident[:, :], 0.0).then_inc(ident_zero, 1)
            pool.wait_ge(ident_zero, 1)
            pool.affine_select(out=ident[:, :], in_=ident[:, :], compare_op=ALU.not_equal, fill=1.0, base=0,
                               pattern=[[-1, P]], channel_multiplier=1).then_inc(ident_ok, 1)
            pool.memset(expo[:, :], -0.5)
            pool.memset(eps[:, :], EPS).then_inc(ident_zero, 1)
            pool.wait_ge(ident_zero, 2)

            def inverse_root(b, seen, step, done):
                wait(pool, seen, b + 1)
                pool.tensor_tensor(rstd[:, :], mean_var[:, :, 1], eps[:, :], ALU.add).then_inc(step, 1)
                wait(pool, step, b + 1)
                pool.tensor_tensor(rstd[:, :], rstd[:, :], expo[:, :], ALU.pow).then_inc(done, 1)

            def add_bias(b, bias, done):
                r = resid[:, one(b), :, :].rearrange("p b t d -> p (b t) d")
                pool.tensor_tensor(r, r, bias, ALU.add).then_inc(done, 1)

            def split_qk(b, n):
                hi, lo = ((q_hi, q_lo), (k_hi, k_lo))[n % 2]
                wait(pool, qk_ok, 4 * b + n + 1)
                pool.tensor_tensor(lo[:, :], lo[:, :], hi[:, :].bitcast(F32), ALU.subtract).then_inc(qk_lo_ok, 1)

            def place_values(b):
                for kt in range(T):
                    if kt % 2 == 0:
                        wait(pool, v_next_ok, 2 * b + kt // 2 + 1)
                        if isinstance(b, int) and b == 0:
                            wait(pool, v_ones_ok, 1)
                    wait(pool, pv_ok, T * (UB * b - 1) + kt + 1)
                    v = v_next[:, kt, :].rearrange("p (h d) -> p h d", d=HD)
                    rows = v_ones[:, kt, 0:VH * N_HEADS].rearrange("p (h w) -> p h w", w=VH)
                    one_each = rows[:, :, HD:VH].to_broadcast([P, N_HEADS, HD])
                    pool.tensor_tensor(rows[:, :, 0:HD], v, one_each, ALU.mult).then_inc(v_ok, 1)

            def add_bo(b):
                add_bias(b, bo_eff[:, one(b), :].to_broadcast([P, T, D]), resid_ok)

            def add_b2(b):
                add_bias(b, b2_bc[:, None, :].to_broadcast([P, T, D]), resid2_ok)

            pool.memset(k_stack[64:64 + K_B - K_A + 1, :, :, :].bitcast(F32), 1.0).then_inc(consts_ok, 1)
            pool.wait_ge(consts_ok, 1)
            inverse_root(0, stats_ok, var_eps_ok, rstd_ok)
            pool.wait_ge(rstd_ok, 1)
            pool.memset(q_stack[64:65, :, :, :].bitcast(F32), 0.0).then_inc(consts_ok, 1)
            pool.wait_ge(consts_ok, 2)
            split_qk(0, 0)
            split_qk(0, 1)
            pool.wait_ge(mlp_hi_ok, 2)
            pool.tensor_tensor(w1_lo[:, :, :], w1_raw, w1_hi[:, :, :].bitcast(F32), ALU.subtract).then_inc(mlp_lo_ok, 1)
            pool.tensor_tensor(w2_lo[:, :, :], w2_raw, w2_hi[:, :, :].bitcast(F32), ALU.subtract).then_inc(mlp_lo_ok, 1)

            def batch(i):
                if live(i + 1, B):
                    inverse_root(i + 1, stats_ok, var_eps_ok, rstd_ok)
                elif live(i, B):
                    wait(pool, xhat_ok, B)
                if live(i, B):
                    split_qk(i, 2)
                    split_qk(i, 3)
                    if isinstance(i, int) and i == 0:
                        wait(pool, u_ok, B + 1)
                    add_bo(i)
                    place_values(i)
                if live(i + 1, B):
                    split_qk(i + 1, 0)
                    split_qk(i + 1, 1)

            over_batches(pool, batch)

            inverse_root(0, stats2_ok, var_eps2_ok, rstd2_ok)
            pool.wait_ge(bc_in, 32)

            def mlp(j, _):
                if live(j, B):
                    for f in range(FT):
                        n = FT * j + f
                        if f == 1 and live(j + 1, B):
                            inverse_root(j + 1, stats2_ok, var_eps2_ok, rstd2_ok)
                            add_b2(j)
                        elif f == 1:
                            add_b2(j)
                        wait(pool, h_ok, n + 1)
                        wait(pool, w2_mm, n - HB + 1)
                        pool.tensor_tensor(h_lo[:, f % HB, :], h_full[:, f % HB, :],
                                           h_hi[:, f % HB, :].bitcast(F32), ALU.subtract).then_inc(h_lo_ok, 1)

            over_mlp_batches(pool, mlp)

        @block.scalar
        def _(act):
            for n, w in enumerate((wt_attn, wt_ffn)):
                act.dma_start(wt_raw[:, n, :, :], w.rearrange("(c p) f -> p c f", p=P)).then_inc(wt_in[n], 16)
                act.dma_start(w_raw[:, n, :, :], (wq, wk)[n].rearrange("(c p) f -> p c f", p=P)).then_inc(raw_in, 16)

            def take_x(b, c, bank=work):
                wait(act, x_turned, 2 * b + c + 1)
                wait(act, gain_ok, b + 1)
                act.activation(xm_hi[:, c, :], bank[:, :], ACT.Identity,
                               scale=gain_now[:, 0, c:c + 1]).then_inc(xm_hi_ok, 1)

            def take_qk(b, n, bank=work):
                wait(act, qk_mm, 4 * b + n + 1)
                wait(act, qk_bias_ok, b + 1)
                k = C * (n % 2) + n // 2
                u = UB * b + 2 * (n // 2)
                done = 128 * (u // 2) if isinstance(u, int) else 256 * b + 128 * (n // 2)
                wait(act, stack_in[0], done)
                wait(act, stack_in[1], done)
                act.activation((q_hi, k_hi)[n % 2][:, :], bank[:, :], ACT.Identity,
                               bias=qk_bias_now[:, k:k + 1])
                act.activation((q_lo, k_lo)[n % 2][:, :], bank[:, :], ACT.Identity,
                               bias=qk_bias_now[:, k:k + 1]).then_inc(qk_ok, 1)

            def take_v(b, half):
                wait(act, v_mm, 2 * b + half + 1)
                wait(act, v_ok, T * b)
                act.copy(v_next[:, 2 * half:2 * half + 2, :],
                         work[:, :].rearrange("p (t d) -> p t d", t=2)).then_inc(v_next_ok, 1)

            def take_attn(b, half):
                wait(act, attn_turned, 2 * b + half + 1)
                act.copy(at_hi[:, :, :], work[:, :].rearrange("p (c s) -> p c s", c=C)).then_inc(at_hi_ok, 1)

            def take_pv(u):
                wait(act, pv_ok, T * (u + 1))
                wait(act, pv_turned, u)
                act.copy(pv_sb[:, :], pv[:, :]).then_inc(pv_sb_ok, 1)

            def batch(i):
                for g in range(UB):
                    s = UB * i + g
                    for t in range(TILES):
                        kt, h = t // G, t % G
                        if live(s - LAG, UNITS):
                            u = s - LAG
                            wait(act, shifted_ok, TILES * u + t + 1)
                            if h == 0:
                                wait(act, pv_ok, T * u + kt - 1)
                                if isinstance(u, int) and u == 0 and kt < 2:
                                    wait(act, mlp_lo_ok, 2)
                                    wait(act, bias_ok, 2)
                            act.activation(probs[:, kt % 2, h, :], shifted[t % 2][:, :], ACT.Exp,
                                           scale=float(HD) ** -0.5).then_inc(exp_ok, 1)
                        if t == 3 and live(s - 1, UNITS):
                            wait(act, max_turned, s)
                            if live(s - 2, UNITS):
                                wait(act, max_in[g % 2], (16 * (s - 2 + 2 - g % 2)) if isinstance(s, int)
                                     else 64 * i + 16 * (g - g % 2))
                            act.copy(m_hi[:, :], turn[0:TILES, 0:P]).then_inc(m_hi_ok, 1)
                        if t == 3 and live(s - 3, UNITS):
                            take_pv(s - 3)
                        if live(i, B):
                            if (g, t) in ((0, 4), (0, 8)):
                                take_qk(i, 2 + (t == 8))
                            if (g, t) in ((0, 12), (1, 0)):
                                take_v(i, int(t == 0))
                        if live(i + 1, B):
                            if (g, t) in ((1, 4), (1, 8)):
                                take_x(i + 1, int(t == 8))
                            if (g, t) in ((2, 8), (2, 12)):
                                take_qk(i + 1, int(t == 12))
                        if live(i - 1, B) and (g, t) in ((3, 0), (3, 8)):
                            take_attn(i - 1, int(t == 8))

            def weight_hi(n):
                src, dst = w_raw[:, n, :, :], wqkv["qkvo"[n]][0][:, :, :]
                if n < 2:
                    for c in range(C):
                        for m in range(2):
                            last = act.copy(in_order(dst[:, c, P * m:P * m + P]),
                                            by_head_in_unit(src[:, c, P * m:P * m + P]))
                else:
                    last = act.copy(dst, src)
                last.then_inc(w_hi_ok, 1)

            act.wait_ge(raw_in, 32)
            weight_hi(0)
            weight_hi(1)
            take_x(0, 0)
            take_x(0, 1, shifted[0])
            act.wait_ge(raw_vo_in, 32)
            weight_hi(2)
            weight_hi(3)
            take_qk(0, 0)
            take_qk(0, 1, shifted[1])
            act.wait_ge(mlp_in, 32)
            act.copy(w1_hi[:, :, :], w1_raw).then_inc(mlp_hi_ok, 1)
            act.copy(w2_hi[:, :, :], w2_raw).then_inc(mlp_hi_ok, 1)
            over_batches(act, batch)

            def take_y(j, c, par):
                wait(act, x2_turned, 2 * j + c + 1)
                wait(act, gain2_ok, j + 1)
                act.activation(ym[par][0][:, c, :], (turn, work)[c][:, :], ACT.Identity,
                               scale=gain_now[:, 1, c:c + 1]).then_inc(ym_hi_ok, 1)

            take_y(0, 0, 0)
            take_y(0, 1, 0)

            def store(b):
                wait(act, y_ok, 2 * b + 2)
                act.dma_start(out_v[:, one(b), :], resid[:, one(b), :, :].rearrange(
                    "p b t d -> p b (t d)")).then_inc(stored, 16)

            def mlp(j, par):
                if live(j, B):
                    for f in range(FT):
                        n = FT * j + f
                        wait(act, w1_mm, n + 1)
                        if f == 0:
                            wait(act, b1_ok, j + 1)
                        wait(act, w2_mm, n - HB + 1)
                        act.activation(h_hi[:, f % HB, :], scores[f % 2][:, :], ACT.Gelu,
                                       bias=b1_now[:, par, f:f + 1]).then_inc(h_hi_ok, 1)
                        wait(act, h_lo_ok, n - HB + 1)
                        act.activation(h_full[:, f % HB, :], scores[f % 2][:, :], ACT.Gelu,
                                       bias=b1_now[:, par, f:f + 1]).then_inc(h_ok, 1)
                        if f in (3, 5) and live(j + 1, B):
                            take_y(j + 1, int(f == 5), 1 - par)
                        if f == 4 and live(j - 1, B):
                            store(j - 1)
                elif live(j - 1, B):
                    store(j - 1)

            over_mlp_batches(act, mlp)
            act.wait_ge(stored, 16 * B)

        @block.vector
        def _(dve):
            def take_stats(b, tiles, bn):
                for t in tiles:
                    last = dve.bn_stats(stats[:, t, :], resid[:, one(b), t, :].rearrange("p b d -> p (b d)"))
                if T - 1 in tiles:
                    last.then_inc(bn, 1)

            def mean_variance(b, done):
                for t in range(T):
                    last = dve.bn_aggr(mean_var[:, t, :], stats[:, t, :])
                last.then_inc(done, 1)

            def normalise(b, tiles, root, turned, done):
                if 0 in tiles:
                    wait(dve, root, b + 1)
                    wait(dve, turned, 2 * b)
                for t in tiles:
                    last = dve.tensor_scalar(xhat[:, t, :], resid[:, one(b), t, :].rearrange("p b d -> p (b d)"),
                                             mean_var[:, t, 0:1], rstd[:, t:t + 1], ALU.subtract, ALU.mult)
                if T - 1 in tiles:
                    last.then_inc(done, 1)

            def columns(b):
                wait(dve, xm_lo_ok, 2 * b)
                wait(dve, xm_hi_ok, 2 * b)
                dve.tensor_copy(gain_now[:, 0, :, None], gain[:, 0, :, one(b)]).then_inc(gain_ok, 1)

            def bias_columns(b):
                wait(dve, qk_ok, 4 * b)
                dve.tensor_copy(qk_bias_now[:, :, None], qk_bias[:, :, one(b)]).then_inc(qk_bias_ok, 1)

            def take_x(b, c, bank=work):
                wait(dve, xm_hi_ok, 2 * b + c + 1)
                dve.scalar_tensor_tensor(xm_lo[:, c, :], bank[:, :], gain_now[:, 0, c:c + 1],
                                         xm_hi[:, c, :].bitcast(F32), ALU.mult, ALU.subtract).then_inc(xm_lo_ok, 1)

            def take_attn(b, half):
                wait(dve, at_hi_ok, 2 * b + half + 1)
                dve.tensor_tensor(at_lo[:, :, :], work[:, :].rearrange("p (c s) -> p c s", c=C),
                                  at_hi[:, :, :].bitcast(F32), ALU.subtract).then_inc(at_lo_ok, 1)

            def take_x1(b, half):
                wait(dve, wo_mm, 2 * b + half + 1)
                wait(dve, resid_ok, b + 1)
                r = resid[:, one(b), 2 * half:2 * half + 2, :].rearrange("p b t d -> p (b t) d")
                dve.tensor_tensor(r, work[:, :].rearrange("p (t d) -> p t d", t=2), r, ALU.add).then_inc(x1_ok, 1)

            def take_max(u):
                wait(dve, m_hi_ok, u + 1)
                dve.tensor_tensor(m_lo[:, :], turn[0:TILES, 0:P], m_hi[:, :].bitcast(F32),
                                  ALU.subtract).then_inc(m_lo_ok, 1)

            def take_pv(u, unit, b):
                wait(dve, pv_turned, u + 1)
                tile = turn[:, :].rearrange("p (t h w) -> p t h w", t=T, w=VW)
                dve.reciprocal(recip[:, :, :], tile[:, :, :, HD]).then_inc(recip_ok, 1)
                wait(dve, recip_ok, u + 1)
                if unit == 0:
                    wait(dve, attn_turned, 2 * b)
                dve.tensor_tensor(attn[:, :, unit * G * HD:(unit + 1) * G * HD].rearrange(
                    "p t (h d) -> p t h d", d=HD), tile[:, :, :, 0:HD],
                    recip[:, :, :, None].to_broadcast([P, T, G, HD]), ALU.mult).then_inc(attn_ok, 1)

            def modulation(n, bank, col, mm):
                step = 7 * n
                bt, w, b = (("bt_attn", "ln1_w", "ln1_b"), ("bt_ffn", "ln2_w", "ln2_b"))[n]

                def column(name, count):
                    return vec_cols[:, at[name]:at[name] + count, None].to_broadcast([P, count, B])

                dve.wait_ge(mod_mm, mm)
                dve.tensor_tensor(mod[:, n, :, :], bank[:, col:col + 2 * C * B].rearrange("p (n b) -> p n b", b=B),
                                  column(bt, 2 * C), ALU.add).then_inc(mod_step, 1)
                dve.wait_ge(mod_step, step + 1)
                dve.tensor_scalar(mod[:, n, C:2 * C, :], mod[:, n, C:2 * C, :], 1.0, None,
                                  ALU.add).then_inc(mod_step, 1)
                dve.wait_ge(mod_step, step + 2)
                dve.tensor_tensor(gain[:, n, :, :], mod[:, n, C:2 * C, :], column(w, C), ALU.mult).then_inc(mod_step, 1)
                dve.tensor_tensor(offs[:, n, :, :], mod[:, n, C:2 * C, :], column(b, C), ALU.mult).then_inc(mod_step, 1)
                dve.wait_ge(mod_step, step + 4)
                if n == 0:
                    columns(0)
                dve.tensor_tensor(offs[:, n, :, :], offs[:, n, :, :], mod[:, n, 0:C, :], ALU.add).then_inc(mod_step, 1)
                dve.wait_ge(mod_step, step + 5)
                if n == 0:
                    dve.tensor_copy(offs_hi[:, :, :], offs[:, 0, :, :]).then_inc(mod_step, 1)
                    dve.wait_ge(mod_step, step + 6)
                    dve.tensor_tensor(offs_lo[:, :, :], offs[:, 0, :, :], offs_hi[:, :, :].bitcast(F32),
                                      ALU.subtract).then_inc(mod_step, 1)

            def weight_lo(n):
                dve.wait_ge(w_hi_ok, n + 1)
                src = w_raw[:, n, :, :]
                hi, lo = wqkv["qkvo"[n]][0][:, :, :].bitcast(F32), wqkv["qkvo"[n]][1][:, :, :]
                if n < 2:
                    for c in range(C):
                        for m in range(2):
                            k = slice(P * m, P * m + P)
                            last = dve.tensor_tensor(in_order(lo[:, c, k]), by_head_in_unit(src[:, c, k]),
                                                     in_order(hi[:, c, k]), ALU.subtract)
                else:
                    last = dve.tensor_tensor(lo, src, hi, ALU.subtract)
                last.then_inc(w_lo_ok, 1)

            def take_u(b):
                if b == 0:
                    dve.wait_ge(bc_in, 32)
                dve.wait_ge(u_mm, b + 1)
                dve.tensor_tensor(bo_eff[:, b, :], shifted[b % 2][:, 0:D], bo_bc, ALU.add).then_inc(u_ok, 1)

            def take_b1():
                dve.wait_ge(bias_mm, 3)
                dve.tensor_tensor(b1_eff[:, :, :], pv[:, 0:FT * B].rearrange("p (n b) -> p n b", b=B),
                                  vec_cols[:, at["b1"]:at["b1"] + FT, None].to_broadcast([P, FT, B]),
                                  ALU.add).then_inc(bias_ok, 1)

            dve.memset(v_ones[:, :, :], 1.0).then_inc(v_ones_ok, 1)
            dve.wait_ge(x_in[0], 16)
            take_stats(0, range(T), bn_ok)
            dve.wait_ge(bn_ok, 1)
            mean_variance(0, stats_ok)
            dve.wait_ge(qk_rows_in, 32)
            dve.tensor_copy(in_order(qk_rows_p), by_head_in_unit(qk_rows)).then_inc(rows_perm, 1)
            dve.wait_ge(rows_turned, 1)
            dve.tensor_copy(vec_cols[:, :], turn[:, 0:n_vec + 2 * C]).then_inc(cols_ok, 1)
            dve.tensor_copy(cond_cols[:, :, :].rearrange("p c b -> p (c b)"), turn[:, 64:64 + C * B]).then_inc(cols_ok, 1)
            normalise(0, range(T), rstd_ok, x_turned, xhat_ok)
            dve.wait_ge(cols_ok, 2)
            modulation(0, scores[0], 0, 1)
            weight_lo(0)
            weight_lo(1)
            take_x(0, 0)
            take_x(0, 1, shifted[0])
            dve.wait_ge(bias_mm, 1)
            dve.tensor_tensor(qk_bias[:, :, :], scores[1][:, 0:2 * C * B].rearrange("p (n b) -> p n b", b=B),
                              vec_cols[:, n_vec:n_vec + 2 * C, None].to_broadcast([P, 2 * C, B]),
                              ALU.add).then_inc(bias_ok, 1)
            dve.wait_ge(bias_ok, 1)
            bias_columns(0)
            weight_lo(2)
            weight_lo(3)
            dve.wait_ge(bias_mm, 2)
            dve.tensor_tensor(v_bias[:, :, :], pv[:, VB:VB + C * B].rearrange("p (n b) -> p n b", b=B),
                              vec_cols[:, at["bv"]:at["bv"] + C, None].to_broadcast([P, C, B]),
                              ALU.add).then_inc(u_ok, 1)
            modulation(1, pv, MOD, 2)

            def batch(i):
                for g in range(UB):
                    s = UB * i + g
                    for t in range(TILES):
                        if live(s, UNITS):
                            wait(dve, scores_ok, TILES * s + t + 1)
                            if t == 0:
                                wait(dve, max_turned, s - 1)
                            dve.tensor_reduce(neg_max[:, g % 2, t:t + 1], scores[(TILES * g + t) % 3][:, :], AX.X, ALU.max,
                                              negate=True).then_inc(max_ok, 1)
                        if isinstance(i, int) and i == 0:
                            if s <= 1 and t % 2 == 0 and 1 <= (TILES * g + t) // 2 <= B:
                                take_u((TILES * g + t) // 2 - 1)
                            if (g, t) == (1, 3):
                                take_b1()
                        if t == 5 and live(s - 1, UNITS):
                            take_max(s - 1)
                        if t == TV + 1 and live(s - 3, UNITS):
                            take_pv(s - 3, (g + 1) % UB, i if g == 3 else i - 1)
                        if live(i + 1, B):
                            if (g, t) == (0, 2):
                                wait(dve, x_in[1], 16)
                                if not isinstance(i, int) or i > 0:
                                    wait(dve, x_in[2], 16)
                            if g == 0 and t in (2, 3, 4, 6):
                                take_stats(i + 1, ((2, 3, 4, 6).index(t),), bn_ok)
                            if (g, t) == (0, 7):
                                wait(dve, bn_ok, i + 2)
                                columns(i + 1)
                                mean_variance(i + 1, stats_ok)
                            if g == 0 and t >= TILES - T:
                                normalise(i + 1, (t - TILES + T,), rstd_ok, x_turned, xhat_ok)
                            if (g, t) == (1, 0):
                                bias_columns(i + 1)
                            if (g, t) in ((1, 5), (1, 9)):
                                take_x(i + 1, int(t == 9))
                        if live(i - 1, B):
                            if (g, t) in ((3, 1), (3, 9)):
                                take_attn(i - 1, int(t == 9))
                            if (g, t) in ((3, 5), (3, 13)):
                                take_x1(i - 1, int(t == 13))

            over_batches(dve, batch)

            def columns2(j, par):
                wait(dve, ym_lo_ok, 2 * j)
                wait(dve, ym_hi_ok, 2 * j)
                dve.tensor_copy(gain_now[:, 1, :, None], gain[:, 1, :, one(j)]).then_inc(gain2_ok, 1)
                wait(dve, h_ok, FT * (j - 1))
                dve.tensor_copy(b1_now[:, par, :, None], b1_eff[:, :, one(j)]).then_inc(b1_ok, 1)

            def take_y(j, c, par):
                wait(dve, ym_hi_ok, 2 * j + c + 1)
                dve.scalar_tensor_tensor(ym[par][1][:, c, :], (turn, work)[c][:, :], gain_now[:, 1, c:c + 1],
                                         ym[par][0][:, c, :].bitcast(F32), ALU.mult,
                                         ALU.subtract).then_inc(ym_lo_ok, 1)

            wait(dve, x1_ok, 2)
            take_stats(0, range(T), bn2_ok)
            dve.wait_ge(bn2_ok, 1)
            columns2(0, 0)
            mean_variance(0, stats2_ok)
            normalise(0, range(T), rstd2_ok, x2_turned, xhat2_ok)
            take_y(0, 0, 0)
            take_y(0, 1, 0)

            def mlp(j, par):
                if live(j + 1, B):
                    wait(dve, x1_ok, 2 * j + 4)
                    take_stats(j + 1, range(T), bn2_ok)
                    wait(dve, bn2_ok, j + 2)
                    columns2(j + 1, 1 - par)
                    mean_variance(j + 1, stats2_ok)
                    normalise(j + 1, range(T), rstd2_ok, x2_turned, xhat2_ok)
                if live(j - 1, B):
                    wait(dve, w2_mm, FT * j)
                    wait(dve, resid2_ok, j)
                    for half in range(2):
                        r = resid[:, one(j - 1), 2 * half:2 * half + 2, :].rearrange("p b t d -> p (b t) d")
                        dve.tensor_tensor(r, sums[1 - par][half][:, :].rearrange("p (t d) -> p t d", t=2), r,
                                          ALU.add).then_inc(y_ok, 1)
                if live(j + 1, B):
                    for c in range(C):
                        take_y(j + 1, c, 1 - par)

            over_mlp_batches(dve, mlp)

        @block.tensor
        def _(pe):
            TERMS = ((0, 0), (0, 1), (1, 0))

            def product(dst, lhs, rhs):
                n = len(lhs) * len(TERMS)
                k = 0
                for left, right in zip(lhs, rhs):
                    for a, b in TERMS:
                        last = pe.matmul(dst, left[a], right[b], start=(k == 0), stop=(k == n - 1))
                        k += 1
                return last

            def parts(pair, *index):
                return [p[index] for p in pair]

            ALL = slice(None)
            xm, am = (xm_hi, xm_lo), (at_hi, at_lo)

            def turn_x(b, c, bank=work):
                wait(pe, xhat_ok, b + 1)
                for t in range(T):
                    last = pe.transpose(bank[:, P * t:P * t + P], xhat[:, t, P * c:P * c + P], ident[:, :])
                last.then_inc(x_turned, 1)

            def project_qk(b, n, bank=work):
                w = wqkv["qk"[n % 2]]
                m = n // 2
                product(bank[:, :], [parts(w, ALL, c, slice(P * m, P * m + P)) for c in range(C)],
                        [parts(xm, ALL, c, ALL) for c in range(C)]).then_inc(qk_mm, 1)

            def project_v(b, half):
                for t in range(2):
                    k = P * (2 * half + t)
                    last = product(work[:, D * t:D * t + D], [parts(xm, ALL, c, slice(k, k + P)) for c in range(C)],
                                   [parts(wqkv["v"], ALL, c, ALL) for c in range(C)])
                last.then_inc(v_mm, 1)

            def turn_attn(b, half):
                wait(pe, attn_ok, UB * (b + 1))
                for c in range(C):
                    for t in range(2):
                        k = P * (2 * c + t)
                        last = pe.transpose(work[:, k:k + P], attn[:, 2 * half + t, P * c:P * c + P], ident[:, :])
                last.then_inc(attn_turned, 1)

            def project_out(b, half):
                for t in range(2):
                    k = P * t
                    last = product(work[:, D * t:D * t + D], [parts(am, ALL, c, slice(k, k + P)) for c in range(C)],
                                   [parts(wqkv["o"], ALL, c, ALL) for c in range(C)])
                last.then_inc(wo_mm, 1)

            def turn_max(u, slot):
                wait(pe, max_ok, TILES * (u + 1))
                wait(pe, attn_ok, u - 2)
                pe.transpose(turn[0:TILES, 0:P], neg_max[:, slot, :], ident[:, :]).then_inc(max_turned, 1)

            def turn_pv(u):
                wait(pe, pv_sb_ok, u + 1)
                if live(u + LAG, UNITS):
                    wait(pe, m_lo_ok, u + LAG + 1)
                else:
                    wait(pe, attn_ok, u)
                for t in range(T):
                    last = pe.transpose(turn[:, P * t:P * t + P], pv_sb[:, P * t:P * t + P], ident[:, :])
                last.then_inc(pv_turned, 1)

            def sum_values(u, unit, kt, b):
                wait(pe, exp_ok, TILES * u + G * kt + G)
                if unit == 0:
                    wait(pe, v_ok, T * b + kt + 1)
                if kt == 0:
                    wait(pe, pv_sb_ok, u)
                for h in range(G):
                    last = pe.matmul(pv[VW * h:VW * h + VW, :], v_ones[:, kt, VH * (G * unit + h):VH * (G * unit + h) + VW],
                                     probs[:, kt % 2, h, :], start=(kt == 0), stop=(kt == T - 1))
                last.then_inc(pv_ok, 1)

            def batch(i):
                for g in range(UB):
                    s = UB * i + g
                    for t in range(TILES):
                        if live(s, UNITS):
                            if t == 0:
                                wait(pe, stack_in[g % 2], 128 * (s // 2 + 1) if isinstance(s, int)
                                     else 256 * i + 128 * (g // 2 + 1))
                            n = TILES * g + t
                            wait(pe, max_ok, TILES * UB * i + n + 1 - (1 if n == 0 else 4 if n < 3 else 3))
                            h, qt = t // T, t % T
                            pe.matmul(scores[n % 3][:, :], q_stack[0:K_A, g, h, P * qt:P * qt + P],
                                      k_stack[0:K_A, g, h, :], start=True, stop=True).then_inc(scores_ok, 1)
                        if live(s - LAG, UNITS):
                            u, slot = s - LAG, (g + LAG) % UB
                            if t == 0:
                                wait(pe, max_in[slot % 2], 32 * (u // 2 + 1) if isinstance(u, int)
                                     else 64 * i + 32 * (g // 2))
                            wait(pe, exp_ok, TILES * u + t - 1)
                            kt, h = t // G, t % G
                            pe.matmul(shifted[t % 2][:, :], k_stack[0:K_B, slot, h, P * kt:P * kt + P],
                                      q_stack[0:K_B, slot, h, :], start=True, stop=True).then_inc(shifted_ok, 1)
                        if isinstance(i, int) and i == 0:
                            if g == 0 and t % 2 == 1:
                                value_bias(t // 2)
                            if (g, t) == (1, 1):
                                hidden_bias()
                            if (g, t) == (1, TILES - 1):
                                pe.wait_ge(u_ok, B + 1)
                                pe.wait_ge(bias_ok, 2)
                            if (g, t) == (0, 12):
                                pe.wait_ge(w_lo_ok, 4)
                        if t % G == 0:
                            project(i, g, t)
                        if t == 2 and live(s - 1, UNITS):
                            turn_max(s - 1, (g + 1) % 2)
                        if t == 2 and live(s - 3, UNITS):
                            sum_values(s - 3, (g + 1) % UB, T - 1, i if g == 3 else i - 1)
                        if t in (6, 10, 14) and live(s - LAG, UNITS):
                            sum_values(s - LAG, (g + LAG) % UB, (t - 6) // G, i if g >= LAG else i - 1)
                        if t == TV and live(s - 3, UNITS):
                            turn_pv(s - 3)
                        if (g, t) == (3, TILES - 1) and live(i - 1, B):
                            wait(pe, x1_ok, 2 * i)

            def value_bias(b):
                pe.wait_ge(u_ok, max(1, b))
                for c in range(C):
                    last = pe.matmul(shifted[b % 2][:, 0:D], v_bias[:, c, b:b + 1].to_broadcast([P, P]),
                                     w_raw[:, 3, c, :], start=(c == 0), stop=(c == C - 1))
                last.then_inc(u_mm, 1)

            def hidden_bias():
                pe.wait_ge(mlp_in, 32)
                pe.wait_ge(mod_step, 12)
                for m in range(FT):
                    for c in range(C):
                        last = pe.matmul(pv[:, B * m:B * m + B], w1_raw[:, c, P * m:P * m + P], offs[:, 1, c, :],
                                         start=(c == 0), stop=(c == C - 1))
                last.then_inc(bias_mm, 1)

            def project(i, g, t):
                if live(i, B):
                    if (g, t) == (0, 4):
                        wait(pe, qk_ok, 4 * i + 2)
                        project_qk(i, 2)
                    if (g, t) == (0, 8):
                        wait(pe, qk_ok, 4 * i + 3)
                        project_qk(i, 3)
                    if (g, t) == (0, 12):
                        wait(pe, qk_ok, 4 * i + 4)
                        project_v(i, 0)
                    if (g, t) == (1, 0):
                        wait(pe, v_next_ok, 2 * i + 1)
                        project_v(i, 1)
                if live(i + 1, B):
                    if (g, t) == (1, 4):
                        wait(pe, v_next_ok, 2 * i + 2)
                        turn_x(i + 1, 0)
                    if (g, t) == (1, 8):
                        wait(pe, xm_lo_ok, 2 * i + 3)
                        turn_x(i + 1, 1)
                    if (g, t) == (2, 8):
                        wait(pe, xm_lo_ok, 2 * i + 4)
                        project_qk(i + 1, 0)
                    if (g, t) == (2, 12):
                        wait(pe, qk_ok, 4 * i + 5)
                        project_qk(i + 1, 1)
                if live(i - 1, B):
                    if (g, t) == (3, 0):
                        if live(i + 1, B):
                            wait(pe, qk_ok, 4 * i + 6)
                        else:
                            wait(pe, v_next_ok, 2 * B)
                        turn_attn(i - 1, 0)
                    if (g, t) == (3, 4):
                        wait(pe, at_lo_ok, 2 * i - 1)
                        project_out(i - 1, 0)
                    if (g, t) == (3, 8):
                        wait(pe, x1_ok, 2 * i - 1)
                        turn_attn(i - 1, 1)
                    if (g, t) == (3, 12):
                        wait(pe, at_lo_ok, 2 * i)
                        project_out(i - 1, 1)

            pe.wait_ge(ident_ok, 1)
            pe.wait_ge(cond_in, 16)
            pe.wait_ge(vec_in, 16 * len(vectors))
            pe.wait_ge(rows_perm, 1)
            pe.transpose(turn[:, 0:n_vec], vec_rows, ident[0:n_vec, 0:n_vec])
            pe.transpose(turn[:, n_vec:n_vec + 2 * C], qk_rows_p, ident[0:2 * C, 0:2 * C])
            for c in range(C):
                last = pe.transpose(turn[:, 64 + B * c:64 + B * c + B], attn[0:B, 3, P * c:P * c + P],
                                    ident[0:B, 0:B])
            last.then_inc(rows_turned, 1)
            pe.wait_ge(cols_ok, 2)

            def modulation(n, bank, col):
                pe.wait_ge(wt_in[n], 16)
                for m in range(2 * C):
                    for c in range(C):
                        k = col + B * m
                        last = pe.matmul(bank[:, k:k + B], wt_raw[:, n, c, P * m:P * m + P], cond_cols[:, c, :],
                                         start=(c == 0), stop=(c == C - 1))
                last.then_inc(mod_mm, 1)

            modulation(0, scores[0], 0)
            turn_x(0, 0)
            turn_x(0, 1, shifted[0])
            pe.wait_ge(mod_step, 7)
            pe.wait_ge(w_lo_ok, 2)
            for n in range(2):
                for m in range(C):
                    k = B * (C * n + m)
                    last = product(scores[1][:, k:k + B], [parts(wqkv["qk"[n]], ALL, c, slice(P * m, P * m + P))
                                                           for c in range(C)],
                                   [parts((offs_hi, offs_lo), ALL, c, ALL) for c in range(C)])
            last.then_inc(bias_mm, 1)
            pe.wait_ge(xm_lo_ok, 2)
            project_qk(0, 0)
            project_qk(0, 1, shifted[1])
            modulation(1, pv, MOD)
            pe.wait_ge(raw_vo_in, 32)
            for m in range(C):
                for c in range(C):
                    k = VB + B * m
                    last = pe.matmul(pv[:, k:k + B], w_raw[:, 2, c, P * m:P * m + P], offs[:, 0, c, :],
                                     start=(c == 0), stop=(c == C - 1))
            last.then_inc(bias_mm, 1)
            pe.wait_ge(bias_ok, 1)
            pe.wait_ge(qk_ok, 2)
            pe.wait_ge(consts_ok, 2)
            over_batches(pe, batch)

            def turn_y(j, c):
                wait(pe, xhat2_ok, j + 1)
                wait(pe, ym_lo_ok, 2 * j - 1 + c)
                for t in range(T):
                    last = pe.transpose((turn, work)[c][:, P * t:P * t + P], xhat[:, t, P * c:P * c + P],
                                        ident[:, :])
                last.then_inc(x2_turned, 1)

            turn_y(0, 0)
            turn_y(0, 1)
            pe.wait_ge(mlp_lo_ok, 2)

            def down(j, par, f):
                wait(pe, h_lo_ok, FT * j + f + 1)
                for t in range(T):
                    acc = sums[par][t // 2][:, D * (t % 2):D * (t % 2) + D]
                    for n, (a, b) in enumerate(TERMS):
                        last = pe.matmul(acc, (h_hi, h_lo)[a][:, f % HB, P * t:P * t + P], (w2_hi, w2_lo)[b][:, f, :],
                                         start=(f == 0 and n == 0 and t % 2 == 0), stop=(f == FT - 1 and n == 2),
                                         skip_group_check=True)
                last.then_inc(w2_mm, 1)

            def mlp(j, par):
                for f in range(FT):
                    n = FT * j + f
                    if live(j, B):
                        if f == 0:
                            wait(pe, ym_lo_ok, 2 * j + 2)
                        wait(pe, h_ok, n - 1)
                        product(scores[f % 2][:, :], [parts((w1_hi, w1_lo), ALL, c, slice(P * f, P * f + P))
                                                      for c in range(C)],
                                [[y[:, c, :] for y in ym[par]] for c in range(C)]).then_inc(w1_mm, 1)
                    if f >= 2 and live(j, B):
                        down(j, par, f - 2)
                    if f < 2 and live(j - 1, B):
                        down(j - 1, 1 - par, FT - 2 + f)
                    if f in (3, 5) and live(j + 1, B):
                        turn_y(j + 1, int(f == 5))
                    if f == FT - 1 and live(j - 1, B):
                        wait(pe, y_ok, 2 * j)

            over_mlp_batches(pe, mlp)


_PRE = "L0_cond_"
_INS = ["x", "cond_1024"] + [_PRE + n for n in (
    "ln1_w", "ln1_b", "ln2_w", "ln2_b", "wq", "bq", "wk", "bk", "wv", "bv", "wo", "bo",
    "wt_attn", "bt_attn", "wt_ffn", "bt_ffn", "w1", "b1", "w2", "b2")]


def kernel(**inputs):
    import numpy as _np
    import concourse.bacc as _bacc
    from concourse import mybir as _mybir
    from concourse.bass_utils import run_bass_kernel_spmd as _run

    nc = _bacc.Bacc("TRN2", target_bir_lowering=False, num_devices=1)
    arrays, args = {}, []
    for name in _INS:
        a = _np.ascontiguousarray(inputs[name])
        arrays[f"in_{name}_dram"] = a
        args.append(nc.dram_tensor(f"in_{name}_dram", a.shape, _mybir.dt.from_np(a.dtype), kind="ExternalInput").ap())
    shape = inputs["x"].shape
    args.append(nc.dram_tensor("out_0_dram", shape, _mybir.dt.float32, kind="ExternalOutput").ap())
    cond_transformer_block(nc, *args)
    r = _run(nc, [arrays], core_ids=[0])
    return r.results[0]["out_0_dram"]
```

```python
from contextlib import ExitStack

import concourse.bass as bass
from concourse import mybir

F32 = mybir.dt.float32
F32R = mybir.dt.float32r
ALU = mybir.AluOpType
ACT = mybir.ActivationFunctionType
AX = mybir.AxisListType

P = 128
N_HEADS = 16
EPS = 1e-5


def cond_transformer_block(nc, x, cond, ln1_w, ln1_b, ln2_w, ln2_b, wq, bq, wk, bk, wv, bv, wo, bo,
                           wt_attn, bt_attn, wt_ffn, bt_ffn, w1, b1, w2, b2, out):
    B, S, D = x.shape
    F = w1.shape[1]
    HD = D // N_HEADS
    T = S // P
    C = D // P
    FT = F // P
    G = 4
    UB = N_HEADS // G
    UNITS = B * UB
    TILES = G * T
    LAG = 2
    K_A = 4 * HD + 1
    K_B = K_A + 2
    VH = HD + 1
    VW = 32
    TV = 8
    HB = 4
    assert S == 512 and D == 256 and HD == 16 and F == 1024

    with ExitStack() as ctx:
        def sb(name, shape, dt=F32):
            return ctx.enter_context(nc.sbuf_tensor(name, shape, dt))

        def sem(name):
            return ctx.enter_context(nc.semaphore(name))

        resid = sb("resid", [P, B, T, D])
        wqkv = {}
        for n in ("q", "k", "v", "o"):
            wqkv[n] = (sb(f"w{n}_hi", [P, C, D], F32R), sb(f"w{n}_lo", [P, C, D], F32R))
        w1_hi, w1_lo = sb("w1_hi", [P, C, F], F32R), sb("w1_lo", [P, C, F], F32R)
        w2_hi, w2_lo = sb("w2_hi", [P, FT, D], F32R), sb("w2_lo", [P, FT, D], F32R)
        q_stack = sb("q_stack", [P, UB, G, S], F32R)
        k_stack = sb("k_stack", [P, UB, G, S], F32R)
        probs = sb("probs", [P, 2, G, S])
        v_ones = sb("v_ones", [P, T, VH * N_HEADS + VW - VH])
        with nc.sbuf_tensor("xhat", [P, T, D], F32) as xhat:
            pass
        at_hi, at_lo = sb("at_hi", [P, C, S // 2], F32R), sb("at_lo", [P, C, S // 2], F32R)
        xm_hi, xm_lo = sb("xm_hi", [P, C, S], F32R), sb("xm_lo", [P, C, S], F32R)
        q_hi, q_lo = sb("q_hi", [P, S], F32R), sb("q_lo", [P, S])
        k_hi, k_lo = sb("k_hi", [P, S], F32R), sb("k_lo", [P, S])
        pv_sb = sb("pv_sb", [P, S])
        attn = sb("attn", [P, T, D])
        v_next = sb("v_next", [P, T, D])
        bo_bc, b2_bc = sb("bo_bc", [P, D]), sb("b2_bc", [P, D])
        ident = sb("ident", [P, P])
        neg_max = sb("neg_max", [P, 2, TILES])
        m_hi, m_lo = sb("m_hi", [TILES, P], F32R), sb("m_lo", [TILES, P], F32R)
        recip = sb("recip", [P, T, G])
        stats = sb("stats", [P, T, 6])
        mean_var = sb("mean_var", [P, T, 2])
        rstd, eps, expo = sb("rstd", [P, T]), sb("eps", [P, T]), sb("expo", [P, T])
        n_vec = 4 * C + C + 2 * 2 * C + FT
        vec_cols = sb("vec_cols", [P, n_vec + 2 * C])
        cond_cols = sb("cond_cols", [P, C, B])
        mod = sb("mod", [P, 2, 2 * C, B])
        gain = sb("gain", [P, 2, C, B])
        offs = sb("offs", [P, 2, C, B])
        offs_hi, offs_lo = sb("offs_hi", [P, C, B], F32R), sb("offs_lo", [P, C, B], F32R)
        qk_bias = sb("qk_bias", [P, 2 * C, B])
        v_bias = sb("v_bias", [P, C, B])
        b1_eff = sb("b1_eff", [P, FT, B])
        gain_now = sb("gain_now", [P, 2, C])
        qk_bias_now = sb("qk_bias_now", [P, 2 * C])
        v_bias_now = sb("v_bias_now", [P, C])
        b1_now = sb("b1_now", [P, 2, FT])

        w_raw = resid[:, 4:6, :, :].rearrange("p b t d -> p (b t) d").rearrange("p (n c) d -> p n c d", c=C)
        wt_raw = resid[:, 6:8, :, :].rearrange("p b t d -> p b (t d)").rearrange("p n (c f) -> p n c f", c=C)
        vec_rows, qk_rows, qk_rows_p = attn[0:n_vec, 0, 0:P], attn[0:2 * C, 1, 0:P], attn[0:2 * C, 2, 0:P]
        cond_rows = attn[0:B, 3, :]
        probs_flat = probs[:, :, :, :].rearrange("p a g s -> p (a g s)")
        w1_raw = probs_flat[:, 0:C * F].rearrange("p (c f) -> p c f", c=C)
        w2_raw = probs_flat[:, C * F:C * F + FT * D].rearrange("p (f d) -> p f d", f=FT)
        h_full = probs[:, 0, :, :]
        h_hi = q_stack[:, 0, :, :]
        h_lo = q_stack[:, 1, :, :]
        ym = [(xm_hi[:, :, :], xm_lo[:, :, :]), (k_stack[:, 0, 0:C, :], k_stack[:, 1, 0:C, :])]

        VB, MOD = FT * B, FT * B + C * B

        scores = [ctx.enter_context(nc.psum_tensor(f"scores{n}", [P, S], F32)) for n in range(3)]
        shifted = [ctx.enter_context(nc.psum_tensor(f"shifted{n}", [P, S], F32)) for n in range(2)]
        pv = ctx.enter_context(nc.psum_tensor("pv", [P, S], F32))
        turn = ctx.enter_context(nc.psum_tensor("turn", [P, S], F32))
        work = ctx.enter_context(nc.psum_tensor("work", [P, S], F32))

        sums = [shifted, (scores[2], pv)]

        x_in = [sem("x0_in"), sem("x1_in"), sem("x4_in")]
        vec_in, cond_in = sem("vec_in"), sem("cond_in")
        wt_in, raw_in, raw_vo_in = [sem("wt_attn_in"), sem("wt_ffn_in")], sem("raw_qk_in"), sem("raw_vo_in")
        mlp_in, bc_in, qk_rows_in = sem("mlp_in"), sem("bc_in"), sem("qk_rows_in")
        ident_zero, ident_ok, consts_ok = sem("ident_zero"), sem("ident_ok"), sem("consts_ok")
        rows_turned, cols_ok, mod_mm, mod_step = sem("rows_turned"), sem("cols_ok"), sem("mod_mm"), sem("mod_step")
        rows_perm, v_ones_ok = sem("rows_perm"), sem("v_ones_ok")
        bias_mm, bias_ok, v_bias_ok = sem("bias_mm"), sem("bias_ok"), sem("v_bias_ok")
        w_hi_ok, w_lo_ok, mlp_hi_ok, mlp_lo_ok = sem("w_hi_ok"), sem("w_lo_ok"), sem("mlp_hi_ok"), sem("mlp_lo_ok")
        stack_in = [sem("stack_even_in"), sem("stack_odd_in")]
        max_in = [sem("max_even_in"), sem("max_odd_in")]
        scores_ok, shifted_ok, pv_ok = sem("scores_ok"), sem("shifted_ok"), sem("pv_ok")
        max_turned, pv_turned = sem("max_turned"), sem("pv_turned")
        qk_mm, v_mm, x_turned, attn_turned, wo_mm = (sem("qk_mm"), sem("v_mm"), sem("x_turned"),
                                                     sem("attn_turned"), sem("wo_mm"))
        max_ok, m_lo_ok, xm_lo_ok = sem("max_ok"), sem("m_lo_ok"), sem("xm_lo_ok")
        recip_ok, attn_ok, at_lo_ok, x1_ok = sem("recip_ok"), sem("attn_ok"), sem("at_lo_ok"), sem("x1_ok")
        bn_ok, stats_ok, xhat_ok = sem("bn_ok"), sem("stats_ok"), sem("xhat_ok")
        gain_ok, qk_bias_ok, gain2_ok, b1_ok = sem("gain_ok"), sem("qk_bias_ok"), sem("gain2_ok"), sem("b1_ok")
        exp_ok, m_hi_ok, qk_ok, xm_hi_ok = sem("exp_ok"), sem("m_hi_ok"), sem("qk_ok"), sem("xm_hi_ok")
        pv_sb_ok, at_hi_ok, v_next_ok = sem("pv_sb_ok"), sem("at_hi_ok"), sem("v_next_ok")
        var_eps_ok, rstd_ok, resid_ok, v_ok = sem("var_eps_ok"), sem("rstd_ok"), sem("resid_ok"), sem("v_ok")
        qk_lo_ok = sem("qk_lo_ok")
        bn2_ok, stats2_ok, xhat2_ok = sem("bn2_ok"), sem("stats2_ok"), sem("xhat2_ok")
        var_eps2_ok, rstd2_ok = sem("var_eps2_ok"), sem("rstd2_ok")
        resid2_ok, x2_turned, ym_hi_ok, ym_lo_ok = (sem("resid2_ok"), sem("x2_turned"), sem("ym_hi_ok"),
                                                    sem("ym_lo_ok"))
        w1_mm, h_hi_ok, h_ok, h_lo_ok, w2_mm, y_ok, stored = (sem("w1_mm"), sem("h_hi_ok"), sem("h_ok"),
                                                              sem("h_lo_ok"), sem("w2_mm"), sem("y_ok"),
                                                              sem("stored"))

        x_v = x.rearrange("b (p t) d -> p b (t d)", t=T)
        out_v = out.rearrange("b (p t) d -> p b (t d)", t=T)

        def live(n, end):
            return not isinstance(n, int) or 0 <= n < end

        def wait(eng, s, value):
            if not isinstance(value, int) or value > 0:
                eng.wait_ge(s, value)

        def bank_of(n):
            return {TILES * UB - 2: 0, TILES * UB - 1: 2}.get(n, n % 3)

        def bank_age(n):
            return next(k for k in range(1, 5) if bank_of((n - k) % (TILES * UB)) == bank_of(n))

        def shifted_ring(i):
            return shifted if live(i, B) else shifted + scores[0:2]

        def steps(i):
            return UB if live(i, B) else UB - 1

        def over_batches(eng, body):
            body(0)
            with eng.Fori(1, B - 1) as i:
                body(i)
            body(B - 1)
            body(B)

        def over_mlp_batches(eng, body):
            body(0, 0)
            with eng.Fori(0, B // 2 - 1) as k:
                body(2 * k + 1, 1)
                body(2 * k + 2, 0)
            body(B - 1, 1)
            body(B, 0)

        def turn_at(j):
            return (6, 7) if isinstance(j, int) and j == 0 else (3, 5)

        at = {}
        row = 0
        vectors = [("ln1_w", ln1_w, C), ("ln1_b", ln1_b, C), ("ln2_w", ln2_w, C), ("ln2_b", ln2_b, C),
                   ("bv", bv, C), ("bt_attn", bt_attn, 2 * C), ("bt_ffn", bt_ffn, 2 * C), ("b1", b1, FT)]
        for name, _, n in vectors:
            at[name] = row
            row += n
        assert row == n_vec

        def by_head_in_unit(ap):
            return ap.rearrange("p (u h d) -> p u d h", u=2, h=G)

        def in_order(ap):
            return ap.rearrange("p (u d h) -> p u d h", u=2, h=G)

        block = ctx.enter_context(nc.Block())

        @block.sync
        def _(sp):
            sp.dma_start(resid[:, 0, :, :], x_v[:, 0, :].rearrange("p (t d) -> p t d", t=T)).then_inc(x_in[0], 16)
            sp.dma_start(cond_rows, cond).then_inc(cond_in, 16)
            for name, v, n in vectors:
                sp.dma_start(attn[at[name]:at[name] + n, 0, 0:P],
                             v.rearrange("(n p) -> n p", p=P)).then_inc(vec_in, 16)
            sp.dma_start(attn[0:C, 1, 0:P], bq.rearrange("(n p) -> n p", p=P)).then_inc(qk_rows_in, 16)
            sp.dma_start(attn[C:2 * C, 1, 0:P], bk.rearrange("(n p) -> n p", p=P)).then_inc(qk_rows_in, 16)
            for n, w in ((2, wv), (3, wo)):
                sp.dma_start(w_raw[:, n, :, :], w.rearrange("(c p) f -> p c f", p=P)).then_inc(raw_vo_in, 16)
            sp.dma_start(bo_bc[:, :], bo.rearrange("(a d) -> a d", a=1).to_broadcast([P, D])).then_inc(bc_in, 16)
            sp.dma_start(b2_bc[:, :], b2.rearrange("(a d) -> a d", a=1).to_broadcast([P, D])).then_inc(bc_in, 16)
            sp.dma_start(w1_raw, w1.rearrange("(c p) f -> p c f", p=P)).then_inc(mlp_in, 16)
            sp.dma_start(w2_raw, w2.rearrange("(f p) d -> p f d", p=P)).then_inc(mlp_in, 16)
            sp.dma_start(resid[:, 1:4, :, :],
                         x_v[:, 1:4, :].rearrange("p b (t d) -> p b t d", t=T)).then_inc(x_in[1], 16)

            def batch(i):
                for g in range(steps(i)):
                    u = UB * i + g + 1
                    slot, m = (g + 1) % UB, ((g + 1) % UB) // 2
                    if live(u, UNITS):
                        load_stacks(u, slot, i if g + 1 < UB else i + 1, m)
                    if live(u - 2, UNITS):
                        load_max(u - 2, (g - 1) % UB)
                    if isinstance(i, int) and (i, g) == (0, 2):
                        sp.wait_ge(bias_ok, 3)
                        sp.wait_ge(w_lo_ok, 4)
                        sp.dma_start(resid[:, 4:B, :, :],
                                     x_v[:, 4:B, :].rearrange("p b (t d) -> p b t d", t=T)).then_inc(x_in[2], 16)

            def load_stacks(u, slot, b, m):
                split, freed = [4 * b + 2 * m + 1, 4 * b + 2 * m + 2], TILES * (u - UB + 1)
                if not isinstance(u, int):
                    split, freed = [sp.to_reg(n) for n in split], sp.to_reg(freed)
                wait(sp, shifted_ok, freed)
                rows = slice(64 * (slot % 2), 64 * (slot % 2) + 64)
                qh, kh = q_hi[:, :].bitcast(F32), k_hi[:, :].bitcast(F32)
                for stack, parts, count in ((q_stack, (qh, qh, q_lo, q_lo), split[0]),
                                            (k_stack, (kh, k_lo, kh, k_lo), split[1])):
                    wait(sp, qk_lo_ok, count)
                    for n, part in enumerate(parts):
                        sp.dma_start(stack[HD * n:HD * n + HD, slot, :, :].bitcast(F32),
                                     part[rows, :]).then_inc(stack_in[slot % 2], 16)

            def load_max(u, slot):
                wait(sp, m_lo_ok, u + 1)
                for n, part in enumerate((m_hi, m_lo)):
                    sp.dma_start(q_stack[K_A + n:K_A + n + 1, slot, :, :].bitcast(F32),
                                 part[:, :].bitcast(F32)).then_inc(max_in[slot % 2], 16)

            load_stacks(0, 0, 0, 0)
            over_batches(sp, batch)

        def one(i):
            return slice(i, i + 1) if isinstance(i, int) else bass.ds(i, 1)

        @block.gpsimd
        def _(pool):
            pool.memset(ident[:, :], 0.0).then_inc(ident_zero, 1)
            pool.wait_ge(ident_zero, 1)
            pool.affine_select(out=ident[:, :], in_=ident[:, :], compare_op=ALU.not_equal, fill=1.0, base=0,
                               pattern=[[-1, P]], channel_multiplier=1).then_inc(ident_ok, 1)
            pool.memset(expo[:, :], -0.5)
            pool.memset(eps[:, :], EPS).then_inc(ident_zero, 1)
            pool.wait_ge(ident_zero, 2)

            def inverse_root(b, seen, step, done):
                wait(pool, seen, b + 1)
                pool.tensor_tensor(rstd[:, :], mean_var[:, :, 1], eps[:, :], ALU.add).then_inc(step, 1)
                wait(pool, step, b + 1)
                pool.tensor_tensor(rstd[:, :], rstd[:, :], expo[:, :], ALU.pow).then_inc(done, 1)

            def add_bias(b, bias, done):
                r = resid[:, one(b), :, :].rearrange("p b t d -> p (b t) d")
                pool.tensor_tensor(r, r, bias, ALU.add).then_inc(done, 1)

            def split_qk(b, n):
                hi, lo = ((q_hi, q_lo), (k_hi, k_lo))[n % 2]
                wait(pool, qk_ok, 4 * b + n + 1)
                pool.tensor_tensor(lo[:, :], lo[:, :], hi[:, :].bitcast(F32), ALU.subtract).then_inc(qk_lo_ok, 1)

            def place_values(b):
                for kt in range(T):
                    if kt % 2 == 0:
                        wait(pool, v_next_ok, 2 * b + kt // 2 + 1)
                        if isinstance(b, int) and b == 0:
                            wait(pool, v_ones_ok, 1)
                    wait(pool, pv_ok, T * (UB * b - 1) + kt + 1)
                    v = v_next[:, kt, :].rearrange("p (h d) -> p h d", d=HD)
                    rows = v_ones[:, kt, 0:VH * N_HEADS].rearrange("p (h w) -> p h w", w=VH)
                    one_each = rows[:, :, HD:VH].to_broadcast([P, N_HEADS, HD])
                    pool.tensor_tensor(rows[:, :, 0:HD], v, one_each, ALU.mult).then_inc(v_ok, 1)

            def add_bo(b):
                add_bias(b, bo_bc[:, None, :].to_broadcast([P, T, D]), resid_ok)

            def add_b2(b):
                add_bias(b, b2_bc[:, None, :].to_broadcast([P, T, D]), resid2_ok)

            pool.memset(k_stack[64:64 + K_B - K_A + 1, :, :, :].bitcast(F32), 1.0).then_inc(consts_ok, 1)
            pool.wait_ge(consts_ok, 1)
            inverse_root(0, stats_ok, var_eps_ok, rstd_ok)
            pool.wait_ge(rstd_ok, 1)
            pool.memset(q_stack[64:65, :, :, :].bitcast(F32), 0.0).then_inc(consts_ok, 1)
            pool.wait_ge(consts_ok, 2)
            split_qk(0, 0)
            split_qk(0, 1)
            pool.wait_ge(mlp_hi_ok, 2)
            pool.tensor_tensor(w1_lo[:, :, :], w1_raw, w1_hi[:, :, :].bitcast(F32), ALU.subtract).then_inc(mlp_lo_ok, 1)
            pool.tensor_tensor(w2_lo[:, :, :], w2_raw, w2_hi[:, :, :].bitcast(F32), ALU.subtract).then_inc(mlp_lo_ok, 1)

            def batch(i):
                if live(i + 1, B):
                    inverse_root(i + 1, stats_ok, var_eps_ok, rstd_ok)
                elif live(i, B):
                    wait(pool, xhat_ok, B)
                if live(i, B):
                    split_qk(i, 2)
                    split_qk(i, 3)
                    if isinstance(i, int) and i == 0:
                        pool.wait_ge(bc_in, 32)
                    add_bo(i)
                    place_values(i)
                if live(i + 1, B):
                    split_qk(i + 1, 0)
                    split_qk(i + 1, 1)

            over_batches(pool, batch)

            inverse_root(0, stats2_ok, var_eps2_ok, rstd2_ok)

            def mlp(j, _):
                if live(j, B):
                    for f in range(FT):
                        n = FT * j + f
                        if f == 1 and live(j + 1, B):
                            inverse_root(j + 1, stats2_ok, var_eps2_ok, rstd2_ok)
                            add_b2(j)
                        elif f == 1:
                            add_b2(j)
                        wait(pool, h_ok, n + 1)
                        wait(pool, w2_mm, n - HB + 1)
                        pool.tensor_tensor(h_lo[:, f % HB, :], h_full[:, f % HB, :],
                                           h_hi[:, f % HB, :].bitcast(F32), ALU.subtract).then_inc(h_lo_ok, 1)

            over_mlp_batches(pool, mlp)

        @block.scalar
        def _(act):
            for n, w in enumerate((wt_attn, wt_ffn)):
                act.dma_start(wt_raw[:, n, :, :], w.rearrange("(c p) f -> p c f", p=P)).then_inc(wt_in[n], 16)
                act.dma_start(w_raw[:, n, :, :], (wq, wk)[n].rearrange("(c p) f -> p c f", p=P)).then_inc(raw_in, 16)

            def take_x(b, c, bank=work):
                wait(act, x_turned, 2 * b + c + 1)
                wait(act, gain_ok, b + 1)
                act.activation(xm_hi[:, c, :], bank[:, :], ACT.Identity,
                               scale=gain_now[:, 0, c:c + 1]).then_inc(xm_hi_ok, 1)

            def take_qk(b, n, bank=work):
                wait(act, qk_mm, 4 * b + n + 1)
                wait(act, qk_bias_ok, b + 1)
                k = C * (n % 2) + n // 2
                u = UB * b + 2 * (n // 2)
                done = 128 * (u // 2) if isinstance(u, int) else 256 * b + 128 * (n // 2)
                wait(act, stack_in[0], done)
                wait(act, stack_in[1], done)
                act.activation((q_hi, k_hi)[n % 2][:, :], bank[:, :], ACT.Identity,
                               bias=qk_bias_now[:, k:k + 1])
                act.activation((q_lo, k_lo)[n % 2][:, :], bank[:, :], ACT.Identity,
                               bias=qk_bias_now[:, k:k + 1]).then_inc(qk_ok, 1)

            def take_v(b, half):
                wait(act, v_mm, 2 * b + half + 1)
                wait(act, v_ok, T * b)
                act.copy(v_next[:, 2 * half:2 * half + 2, :],
                         work[:, :].rearrange("p (t d) -> p t d", t=2)).then_inc(v_next_ok, 1)

            def take_attn(b, half):
                wait(act, attn_turned, 2 * b + half + 1)
                wait(act, v_bias_ok, b + 1)
                for c in range(C):
                    last = act.activation(at_hi[:, c, :], work[:, S // 2 * c:S // 2 * (c + 1)], ACT.Identity,
                                          bias=v_bias_now[:, c:c + 1])
                last.then_inc(at_hi_ok, 1)

            def take_pv(u):
                wait(act, pv_ok, T * (u + 1))
                wait(act, pv_turned, u)
                act.copy(pv_sb[:, :], pv[:, :]).then_inc(pv_sb_ok, 1)

            def batch(i):
                for g in range(steps(i)):
                    s = UB * i + g
                    for t in range(TILES):
                        kt, h = t // G, t % G
                        if live(s - LAG, UNITS):
                            u = s - LAG
                            wait(act, shifted_ok, TILES * u + t + 1)
                            if h == 0:
                                wait(act, pv_ok, T * u + kt - 1)
                                if isinstance(u, int) and u == 0 and kt < 2:
                                    wait(act, mlp_lo_ok, 2)
                                    wait(act, bias_ok, 3)
                            ring = shifted_ring(i)
                            act.activation(probs[:, kt % 2, h, :], ring[t % len(ring)][:, :], ACT.Exp,
                                           scale=float(HD) ** -0.5).then_inc(exp_ok, 1)
                        if t == 2 and live(s - 1, UNITS):
                            wait(act, max_turned, s)
                            if live(s - 2, UNITS):
                                wait(act, max_in[g % 2], (16 * (s - 2 + 2 - g % 2)) if isinstance(s, int)
                                     else 64 * i + 16 * (g - g % 2))
                            act.copy(m_hi[:, :], turn[0:TILES, 0:P]).then_inc(m_hi_ok, 1)
                        if t == 2 and live(s - 3, UNITS):
                            take_pv(s - 3)
                        if live(i, B):
                            if (g, t) in ((0, 8), (0, 12)):
                                take_qk(i, 2 + ((g, t) == (0, 12)))
                            if (g, t) in ((1, 0), (1, 4)):
                                take_v(i, int((g, t) == (1, 4)))
                        if live(i + 1, B):
                            if (g, t) in ((1, 8), (1, 12)):
                                take_x(i + 1, int((g, t) == (1, 12)))
                            if (g, t) in ((2, 8), (2, 12)):
                                take_qk(i + 1, int((g, t) == (2, 12)))
                        if live(i - 1, B) and (g, t) in ((3, 0), (3, 8)):
                            take_attn(i - 1, int((g, t) == (3, 8)))
                        if not live(i, B) and (g, t) in ((0, 12), (1, 4)):
                            take_y(0, int(t == 4), 0, work)

            def weight_hi(n):
                src, dst = w_raw[:, n, :, :], wqkv["qkvo"[n]][0][:, :, :]
                if n < 2:
                    for c in range(C):
                        for m in range(2):
                            last = act.copy(in_order(dst[:, c, P * m:P * m + P]),
                                            by_head_in_unit(src[:, c, P * m:P * m + P]))
                else:
                    last = act.copy(dst, src)
                last.then_inc(w_hi_ok, 1)

            act.wait_ge(raw_in, 32)
            weight_hi(0)
            weight_hi(1)
            take_x(0, 0)
            take_x(0, 1, shifted[0])
            act.wait_ge(raw_vo_in, 32)
            weight_hi(2)
            weight_hi(3)
            take_qk(0, 0)
            take_qk(0, 1, shifted[1])
            act.wait_ge(mlp_in, 32)
            act.copy(w1_hi[:, :, :], w1_raw).then_inc(mlp_hi_ok, 1)
            act.copy(w2_hi[:, :, :], w2_raw).then_inc(mlp_hi_ok, 1)
            def take_y(j, c, par, bank):
                wait(act, x2_turned, 2 * j + c + 1)
                wait(act, gain2_ok, j + 1)
                act.activation(ym[par][0][:, c, :], bank[:, :], ACT.Identity,
                               scale=gain_now[:, 1, c:c + 1]).then_inc(ym_hi_ok, 1)

            over_batches(act, batch)

            def store(b):
                wait(act, y_ok, 2 * b + 2)
                act.dma_start(out_v[:, one(b), :], resid[:, one(b), :, :].rearrange(
                    "p b t d -> p b (t d)")).then_inc(stored, 16)

            def mlp(j, par):
                if live(j, B):
                    for f in range(FT):
                        n = FT * j + f
                        wait(act, w1_mm, n + 1)
                        if f == 0:
                            wait(act, b1_ok, j + 1)
                        wait(act, w2_mm, n - HB + 1)
                        act.activation(h_hi[:, f % HB, :], scores[f % 2][:, :], ACT.Gelu,
                                       bias=b1_now[:, par, f:f + 1]).then_inc(h_hi_ok, 1)
                        wait(act, h_lo_ok, n - HB + 1)
                        act.activation(h_full[:, f % HB, :], scores[f % 2][:, :], ACT.Gelu,
                                       bias=b1_now[:, par, f:f + 1]).then_inc(h_ok, 1)
                        if isinstance(j, int) and j == 0 and f in (0, 3):
                            take_attn(B - 1, f // 3)
                        if f in turn_at(j) and live(j + 1, B):
                            c = turn_at(j).index(f)
                            take_y(j + 1, c, 1 - par, (turn, work)[c])
                        if f == 4 and live(j - 1, B):
                            store(j - 1)
                elif live(j - 1, B):
                    store(j - 1)

            over_mlp_batches(act, mlp)
            act.wait_ge(stored, 16 * B)

        @block.vector
        def _(dve):
            def take_stats(b, tiles, bn):
                for t in tiles:
                    last = dve.bn_stats(stats[:, t, :], resid[:, one(b), t, :].rearrange("p b d -> p (b d)"))
                if T - 1 in tiles:
                    last.then_inc(bn, 1)

            def mean_variance(b, done):
                for t in range(T):
                    last = dve.bn_aggr(mean_var[:, t, :], stats[:, t, :])
                last.then_inc(done, 1)

            def normalise(b, tiles, root, turned, done):
                if 0 in tiles:
                    wait(dve, root, b + 1)
                    wait(dve, turned, 2 * b)
                for t in tiles:
                    last = dve.tensor_scalar(xhat[:, t, :], resid[:, one(b), t, :].rearrange("p b d -> p (b d)"),
                                             mean_var[:, t, 0:1], rstd[:, t:t + 1], ALU.subtract, ALU.mult)
                if T - 1 in tiles:
                    last.then_inc(done, 1)

            def columns(b):
                wait(dve, xm_lo_ok, 2 * b)
                wait(dve, xm_hi_ok, 2 * b)
                dve.tensor_copy(gain_now[:, 0, :, None], gain[:, 0, :, one(b)]).then_inc(gain_ok, 1)

            def bias_columns(b):
                wait(dve, qk_ok, 4 * b)
                dve.tensor_copy(qk_bias_now[:, :, None], qk_bias[:, :, one(b)]).then_inc(qk_bias_ok, 1)

            def take_x(b, c, bank=work):
                wait(dve, xm_hi_ok, 2 * b + c + 1)
                dve.scalar_tensor_tensor(xm_lo[:, c, :], bank[:, :], gain_now[:, 0, c:c + 1],
                                         xm_hi[:, c, :].bitcast(F32), ALU.mult, ALU.subtract).then_inc(xm_lo_ok, 1)

            def value_bias_columns(b):
                dve.tensor_copy(v_bias_now[:, :, None], v_bias[:, :, one(b)]).then_inc(v_bias_ok, 1)

            def take_attn(b, half):
                wait(dve, at_hi_ok, 2 * b + half + 1)
                for c in range(C):
                    last = dve.scalar_tensor_tensor(at_lo[:, c, :], work[:, S // 2 * c:S // 2 * (c + 1)],
                                                    v_bias_now[:, c:c + 1], at_hi[:, c, :].bitcast(F32),
                                                    ALU.add, ALU.subtract)
                last.then_inc(at_lo_ok, 1)

            def take_x1(b, half):
                wait(dve, wo_mm, 2 * b + half + 1)
                wait(dve, resid_ok, b + 1)
                r = resid[:, one(b), 2 * half:2 * half + 2, :].rearrange("p b t d -> p (b t) d")
                dve.tensor_tensor(r, work[:, :].rearrange("p (t d) -> p t d", t=2), r, ALU.add).then_inc(x1_ok, 1)

            def take_max(u):
                wait(dve, m_hi_ok, u + 1)
                dve.tensor_tensor(m_lo[:, :], turn[0:TILES, 0:P], m_hi[:, :].bitcast(F32),
                                  ALU.subtract).then_inc(m_lo_ok, 1)

            def take_pv(u, unit, b):
                wait(dve, pv_turned, u + 1)
                tile = turn[:, :].rearrange("p (t h w) -> p t h w", t=T, w=VW)
                dve.reciprocal(recip[:, :, :], tile[:, :, :, HD]).then_inc(recip_ok, 1)
                wait(dve, recip_ok, u + 1)
                if unit == 0:
                    wait(dve, attn_turned, 2 * b)
                dve.tensor_tensor(attn[:, :, unit * G * HD:(unit + 1) * G * HD].rearrange(
                    "p t (h d) -> p t h d", d=HD), tile[:, :, :, 0:HD],
                    recip[:, :, :, None].to_broadcast([P, T, G, HD]), ALU.mult).then_inc(attn_ok, 1)

            def modulation(n, bank, col, mm):
                step = 7 * n
                bt, w, b = (("bt_attn", "ln1_w", "ln1_b"), ("bt_ffn", "ln2_w", "ln2_b"))[n]

                def column(name, count):
                    return vec_cols[:, at[name]:at[name] + count, None].to_broadcast([P, count, B])

                dve.wait_ge(mod_mm, mm)
                dve.tensor_tensor(mod[:, n, :, :], bank[:, col:col + 2 * C * B].rearrange("p (n b) -> p n b", b=B),
                                  column(bt, 2 * C), ALU.add).then_inc(mod_step, 1)
                dve.wait_ge(mod_step, step + 1)
                dve.tensor_scalar(mod[:, n, C:2 * C, :], mod[:, n, C:2 * C, :], 1.0, None,
                                  ALU.add).then_inc(mod_step, 1)
                dve.wait_ge(mod_step, step + 2)
                dve.tensor_tensor(gain[:, n, :, :], mod[:, n, C:2 * C, :], column(w, C), ALU.mult).then_inc(mod_step, 1)
                dve.tensor_tensor(offs[:, n, :, :], mod[:, n, C:2 * C, :], column(b, C), ALU.mult).then_inc(mod_step, 1)
                dve.wait_ge(mod_step, step + 4)
                if n == 0:
                    columns(0)
                dve.tensor_tensor(offs[:, n, :, :], offs[:, n, :, :], mod[:, n, 0:C, :], ALU.add).then_inc(mod_step, 1)
                dve.wait_ge(mod_step, step + 5)
                if n == 0:
                    dve.tensor_copy(offs_hi[:, :, :], offs[:, 0, :, :]).then_inc(mod_step, 1)
                    dve.wait_ge(mod_step, step + 6)
                    dve.tensor_tensor(offs_lo[:, :, :], offs[:, 0, :, :], offs_hi[:, :, :].bitcast(F32),
                                      ALU.subtract).then_inc(mod_step, 1)

            def weight_lo(n):
                dve.wait_ge(w_hi_ok, n + 1)
                src = w_raw[:, n, :, :]
                hi, lo = wqkv["qkvo"[n]][0][:, :, :].bitcast(F32), wqkv["qkvo"[n]][1][:, :, :]
                if n < 2:
                    for c in range(C):
                        for m in range(2):
                            k = slice(P * m, P * m + P)
                            last = dve.tensor_tensor(in_order(lo[:, c, k]), by_head_in_unit(src[:, c, k]),
                                                     in_order(hi[:, c, k]), ALU.subtract)
                else:
                    last = dve.tensor_tensor(lo, src, hi, ALU.subtract)
                last.then_inc(w_lo_ok, 1)

            def take_b1():
                dve.wait_ge(bias_mm, 3)
                dve.tensor_tensor(b1_eff[:, :, :], pv[:, 0:FT * B].rearrange("p (n b) -> p n b", b=B),
                                  vec_cols[:, at["b1"]:at["b1"] + FT, None].to_broadcast([P, FT, B]),
                                  ALU.add).then_inc(bias_ok, 1)

            dve.memset(v_ones[:, :, :], 1.0).then_inc(v_ones_ok, 1)
            dve.wait_ge(x_in[0], 16)
            take_stats(0, range(T), bn_ok)
            dve.wait_ge(bn_ok, 1)
            mean_variance(0, stats_ok)
            dve.wait_ge(qk_rows_in, 32)
            dve.tensor_copy(in_order(qk_rows_p), by_head_in_unit(qk_rows)).then_inc(rows_perm, 1)
            dve.wait_ge(rows_turned, 1)
            dve.tensor_copy(vec_cols[:, :], turn[:, 0:n_vec + 2 * C]).then_inc(cols_ok, 1)
            dve.tensor_copy(cond_cols[:, :, :].rearrange("p c b -> p (c b)"), turn[:, 64:64 + C * B]).then_inc(cols_ok, 1)
            normalise(0, range(T), rstd_ok, x_turned, xhat_ok)
            dve.wait_ge(cols_ok, 2)
            modulation(0, scores[0], 0, 1)
            weight_lo(0)
            weight_lo(1)
            take_x(0, 0)
            take_x(0, 1, shifted[0])
            dve.wait_ge(bias_mm, 1)
            dve.tensor_tensor(qk_bias[:, :, :], scores[1][:, 0:2 * C * B].rearrange("p (n b) -> p n b", b=B),
                              vec_cols[:, n_vec:n_vec + 2 * C, None].to_broadcast([P, 2 * C, B]),
                              ALU.add).then_inc(bias_ok, 1)
            dve.wait_ge(bias_ok, 1)
            bias_columns(0)
            weight_lo(2)
            weight_lo(3)
            dve.wait_ge(bias_mm, 2)
            dve.tensor_tensor(v_bias[:, :, :], pv[:, VB:VB + C * B].rearrange("p (n b) -> p n b", b=B),
                              vec_cols[:, at["bv"]:at["bv"] + C, None].to_broadcast([P, C, B]),
                              ALU.add).then_inc(bias_ok, 1)
            modulation(1, pv, MOD, 2)

            def batch(i):
                for g in range(steps(i)):
                    s = UB * i + g
                    for t in range(TILES):
                        if live(s, UNITS):
                            wait(dve, scores_ok, TILES * s + t + 1)
                            if t == 0:
                                wait(dve, max_turned, s - 1)
                            dve.tensor_reduce(neg_max[:, g % 2, t:t + 1], scores[bank_of(TILES * g + t)][:, :], AX.X, ALU.max,
                                              negate=True).then_inc(max_ok, 1)
                        if isinstance(i, int) and i == 0:
                            if (g, t) == (1, 3):
                                take_b1()
                        if t == 5 and live(s - 1, UNITS):
                            take_max(s - 1)
                        if t == TV + 1 and live(s - 3, UNITS):
                            take_pv(s - 3, (g + 1) % UB, i if g == 3 else i - 1)
                        if live(i + 1, B):
                            if (g, t) == (0, 2):
                                wait(dve, x_in[1], 16)
                                if not isinstance(i, int) or i > 0:
                                    wait(dve, x_in[2], 16)
                            if g == 0 and t in (2, 3, 4, 6):
                                take_stats(i + 1, ((2, 3, 4, 6).index(t),), bn_ok)
                            if (g, t) == (0, 7):
                                wait(dve, bn_ok, i + 2)
                                columns(i + 1)
                                mean_variance(i + 1, stats_ok)
                            if g == 0 and t >= TILES - T:
                                normalise(i + 1, (t - TILES + T,), rstd_ok, x_turned, xhat_ok)
                            if (g, t) == (1, 0):
                                bias_columns(i + 1)
                            if (g, t) in ((1, 9), (1, 13)):
                                take_x(i + 1, int((g, t) == (1, 13)))
                        if live(i - 1, B):
                            if (g, t) in ((3, 1), (3, 9)):
                                take_attn(i - 1, int((g, t) == (3, 9)))
                            if (g, t) in ((3, 5), (3, 13)):
                                take_x1(i - 1, int((g, t) == (3, 13)))
                        if live(i - 1, B) and (g, t) == (2, TILES - 1):
                            value_bias_columns(i - 1)
                        if not live(i, B):
                            if (g, t) == (0, 0):
                                take_stats(0, range(T), bn2_ok)
                                dve.wait_ge(bn2_ok, 1)
                                columns2(0, 0)
                                mean_variance(0, stats2_ok)
                            if (g, t) == (0, 8):
                                normalise(0, range(T), rstd2_ok, x2_turned, xhat2_ok)
                            if (g, t) in ((0, 13), (1, 5)):
                                take_y(0, int(t == 5), 0, work)

            def columns2(j, par):
                wait(dve, ym_lo_ok, 2 * j)
                wait(dve, ym_hi_ok, 2 * j)
                dve.tensor_copy(gain_now[:, 1, :, None], gain[:, 1, :, one(j)]).then_inc(gain2_ok, 1)
                wait(dve, h_ok, FT * (j - 1))
                dve.tensor_copy(b1_now[:, par, :, None], b1_eff[:, :, one(j)]).then_inc(b1_ok, 1)

            def take_y(j, c, par, bank):
                wait(dve, ym_hi_ok, 2 * j + c + 1)
                dve.scalar_tensor_tensor(ym[par][1][:, c, :], bank[:, :], gain_now[:, 1, c:c + 1],
                                         ym[par][0][:, c, :].bitcast(F32), ALU.mult,
                                         ALU.subtract).then_inc(ym_lo_ok, 1)

            over_batches(dve, batch)

            def mlp(j, par):
                if live(j + 1, B):
                    take_stats(j + 1, range(T), bn2_ok)
                    wait(dve, bn2_ok, j + 2)
                    columns2(j + 1, 1 - par)
                    mean_variance(j + 1, stats2_ok)
                    if isinstance(j, int) and j == 0:
                        for half in range(2):
                            take_attn(B - 1, half)
                            take_x1(B - 1, half)
                    normalise(j + 1, range(T), rstd2_ok, x2_turned, xhat2_ok)
                if live(j - 1, B):
                    wait(dve, w2_mm, FT * j)
                    wait(dve, resid2_ok, j)
                    for half in range(2):
                        r = resid[:, one(j - 1), 2 * half:2 * half + 2, :].rearrange("p b t d -> p (b t) d")
                        dve.tensor_tensor(r, sums[1 - par][half][:, :].rearrange("p (t d) -> p t d", t=2), r,
                                          ALU.add).then_inc(y_ok, 1)
                if live(j + 1, B):
                    for c in range(C):
                        take_y(j + 1, c, 1 - par, (turn, work)[c])

            over_mlp_batches(dve, mlp)

        @block.tensor
        def _(pe):
            TERMS = ((0, 0), (0, 1), (1, 0))

            def product(dst, lhs, rhs):
                n = len(lhs) * len(TERMS)
                k = 0
                for left, right in zip(lhs, rhs):
                    for a, b in TERMS:
                        last = pe.matmul(dst, left[a], right[b], start=(k == 0), stop=(k == n - 1))
                        k += 1
                return last

            def parts(pair, *index):
                return [p[index] for p in pair]

            ALL = slice(None)
            xm, am = (xm_hi, xm_lo), (at_hi, at_lo)

            def keep_warm(count):
                for _ in range(count):
                    pe.matmul(turn[:, 128:256], ident[:, :], ident[:, :], start=True, stop=True)

            def turn_x(b, c, bank=work):
                wait(pe, xhat_ok, b + 1)
                for t in range(T):
                    last = pe.transpose(bank[:, P * t:P * t + P], xhat[:, t, P * c:P * c + P], ident[:, :])
                last.then_inc(x_turned, 1)

            def project_qk(b, n, bank=work):
                w = wqkv["qk"[n % 2]]
                m = n // 2
                product(bank[:, :], [parts(w, ALL, c, slice(P * m, P * m + P)) for c in range(C)],
                        [parts(xm, ALL, c, ALL) for c in range(C)]).then_inc(qk_mm, 1)

            def project_v(b, half):
                for t in range(2):
                    k = P * (2 * half + t)
                    last = product(work[:, D * t:D * t + D], [parts(xm, ALL, c, slice(k, k + P)) for c in range(C)],
                                   [parts(wqkv["v"], ALL, c, ALL) for c in range(C)])
                last.then_inc(v_mm, 1)

            def turn_attn(b, half):
                wait(pe, attn_ok, UB * (b + 1))
                for c in range(C):
                    for t in range(2):
                        k = P * (2 * c + t)
                        last = pe.transpose(work[:, k:k + P], attn[:, 2 * half + t, P * c:P * c + P], ident[:, :])
                last.then_inc(attn_turned, 1)

            def project_out(b, half):
                for t in range(2):
                    k = P * t
                    last = product(work[:, D * t:D * t + D], [parts(am, ALL, c, slice(k, k + P)) for c in range(C)],
                                   [parts(wqkv["o"], ALL, c, ALL) for c in range(C)])
                last.then_inc(wo_mm, 1)

            def turn_max(u, slot):
                wait(pe, max_ok, TILES * (u + 1))
                wait(pe, attn_ok, u - 2)
                pe.transpose(turn[0:TILES, 0:P], neg_max[:, slot, :], ident[:, :]).then_inc(max_turned, 1)

            def turn_pv(u):
                wait(pe, pv_sb_ok, u + 1)
                if live(u + LAG, UNITS):
                    wait(pe, m_lo_ok, u + LAG + 1)
                else:
                    wait(pe, attn_ok, u)
                for t in range(T):
                    last = pe.transpose(turn[:, P * t:P * t + P], pv_sb[:, P * t:P * t + P], ident[:, :])
                last.then_inc(pv_turned, 1)

            def sum_values(u, unit, kt, b):
                wait(pe, exp_ok, TILES * u + G * kt + G)
                if unit == 0:
                    wait(pe, v_ok, T * b + kt + 1)
                if kt == 0:
                    wait(pe, pv_sb_ok, u)
                for h in range(G):
                    last = pe.matmul(pv[VW * h:VW * h + VW, :], v_ones[:, kt, VH * (G * unit + h):VH * (G * unit + h) + VW],
                                     probs[:, kt % 2, h, :], start=(kt == 0), stop=(kt == T - 1))
                last.then_inc(pv_ok, 1)

            def batch(i):
                for g in range(steps(i)):
                    s = UB * i + g
                    for t in range(TILES):
                        if live(s, UNITS):
                            if t == 0:
                                wait(pe, stack_in[g % 2], 128 * (s // 2 + 1) if isinstance(s, int)
                                     else 256 * i + 128 * (g // 2 + 1))
                            n = TILES * g + t
                            wait(pe, max_ok, TILES * UB * i + n + 1 - bank_age(n))
                            h, qt = t // T, t % T
                            pe.matmul(scores[bank_of(n)][:, :], q_stack[0:K_A, g, h, P * qt:P * qt + P],
                                      k_stack[0:K_A, g, h, :], start=True, stop=True).then_inc(scores_ok, 1)
                        if live(s - LAG, UNITS):
                            u, slot = s - LAG, (g + LAG) % UB
                            if t == 0:
                                wait(pe, max_in[slot % 2], 32 * (u // 2 + 1) if isinstance(u, int)
                                     else 64 * i + 32 * (g // 2))
                            ring = shifted_ring(i)
                            if t == 0 and not live(i, B):
                                wait(pe, max_ok, TILES * UNITS)
                            first = isinstance(i, int) and i == B and g == 0 and t < len(ring)
                            wait(pe, exp_ok, TILES * u - (t == 0) if first else TILES * u + t + 1 - len(ring))
                            kt, h = t // G, t % G
                            pe.matmul(ring[t % len(ring)][:, :], k_stack[0:K_B, slot, h, P * kt:P * kt + P],
                                      q_stack[0:K_B, slot, h, :], start=True, stop=True).then_inc(shifted_ok, 1)
                        if isinstance(i, int) and i == 0:
                            if g == 0 and t % 2 == 1:
                                hidden_bias(t // 2)
                            if g == 1 and t >= 12:
                                keep_warm(2)
                            if (g, t) == (1, TILES - 1):
                                pe.wait_ge(bias_ok, 3)
                            if (g, t) == (1, 0):
                                pe.wait_ge(w_lo_ok, 4)
                        if t % G == 0:
                            project(i, g, t)
                        if not live(i, B) and (g, t) in ((0, 12), (1, 4)):
                            wait(pe, x1_ok, 2 * B - 2)
                            wait(pe, ym_lo_ok, int(t == 4))
                            turn_y(0, int(t == 4), work)
                        if t == 2 and live(s - 1, UNITS):
                            turn_max(s - 1, (g + 1) % 2)
                        if t == 2 and live(s - 3, UNITS):
                            sum_values(s - 3, (g + 1) % UB, T - 1, i if g == 3 else i - 1)
                        if t in (6, 10, 14) and live(s - LAG, UNITS):
                            sum_values(s - LAG, (g + LAG) % UB, (t - 6) // G, i if g >= LAG else i - 1)
                        if t == TV and live(s - 3, UNITS):
                            turn_pv(s - 3)

            def hidden_bias(m):
                pe.wait_ge(mlp_in, 32)
                pe.wait_ge(mod_step, 12)
                for c in range(C):
                    last = pe.matmul(pv[:, B * m:B * m + B], w1_raw[:, c, P * m:P * m + P], offs[:, 1, c, :],
                                     start=(c == 0), stop=(c == C - 1))
                if m == FT - 1:
                    last.then_inc(bias_mm, 1)

            def project(i, g, t):
                if live(i, B):
                    if (g, t) == (0, 8):
                        wait(pe, qk_ok, 4 * i + 2)
                        project_qk(i, 2)
                    if (g, t) == (0, 12):
                        wait(pe, qk_ok, 4 * i + 3)
                        project_qk(i, 3)
                    if (g, t) == (1, 0):
                        wait(pe, qk_ok, 4 * i + 4)
                        project_v(i, 0)
                    if (g, t) == (1, 4):
                        wait(pe, v_next_ok, 2 * i + 1)
                        project_v(i, 1)
                if live(i + 1, B):
                    if (g, t) == (1, 8):
                        wait(pe, v_next_ok, 2 * i + 2)
                        turn_x(i + 1, 0)
                    if (g, t) == (1, 12):
                        wait(pe, xm_lo_ok, 2 * i + 3)
                        turn_x(i + 1, 1)
                    if (g, t) == (2, 8):
                        wait(pe, xm_lo_ok, 2 * i + 4)
                        project_qk(i + 1, 0)
                    if (g, t) == (2, 12):
                        wait(pe, qk_ok, 4 * i + 5)
                        project_qk(i + 1, 1)
                if live(i - 1, B):
                    if (g, t) == (3, 0):
                        if live(i + 1, B):
                            wait(pe, qk_ok, 4 * i + 6)
                        else:
                            wait(pe, v_next_ok, 2 * B)
                        turn_attn(i - 1, 0)
                    if (g, t) == (3, 4):
                        wait(pe, at_lo_ok, 2 * i - 1)
                        project_out(i - 1, 0)
                    if (g, t) == (3, 8):
                        wait(pe, x1_ok, 2 * i - 1)
                        turn_attn(i - 1, 1)
                    if (g, t) == (3, 12):
                        wait(pe, at_lo_ok, 2 * i)
                        project_out(i - 1, 1)

            pe.wait_ge(ident_ok, 1)
            keep_warm(18)
            pe.wait_ge(cond_in, 16)
            pe.wait_ge(vec_in, 16 * len(vectors))
            pe.wait_ge(rows_perm, 1)
            pe.transpose(turn[:, 0:n_vec], vec_rows, ident[0:n_vec, 0:n_vec])
            pe.transpose(turn[:, n_vec:n_vec + 2 * C], qk_rows_p, ident[0:2 * C, 0:2 * C])
            for c in range(C):
                last = pe.transpose(turn[:, 64 + B * c:64 + B * c + B], attn[0:B, 3, P * c:P * c + P],
                                    ident[0:B, 0:B])
            last.then_inc(rows_turned, 1)
            pe.wait_ge(cols_ok, 2)

            def modulation(n, bank, col):
                pe.wait_ge(wt_in[n], 16)
                for m in range(2 * C):
                    for c in range(C):
                        k = col + B * m
                        last = pe.matmul(bank[:, k:k + B], wt_raw[:, n, c, P * m:P * m + P], cond_cols[:, c, :],
                                         start=(c == 0), stop=(c == C - 1))
                last.then_inc(mod_mm, 1)

            modulation(0, scores[0], 0)
            turn_x(0, 0)
            turn_x(0, 1, shifted[0])
            keep_warm(4)
            pe.wait_ge(mod_step, 7)
            pe.wait_ge(w_lo_ok, 2)
            for n in range(2):
                for m in range(C):
                    k = B * (C * n + m)
                    last = product(scores[1][:, k:k + B], [parts(wqkv["qk"[n]], ALL, c, slice(P * m, P * m + P))
                                                           for c in range(C)],
                                   [parts((offs_hi, offs_lo), ALL, c, ALL) for c in range(C)])
            last.then_inc(bias_mm, 1)
            pe.wait_ge(xm_lo_ok, 2)
            project_qk(0, 0)
            project_qk(0, 1, shifted[1])
            modulation(1, pv, MOD)
            pe.wait_ge(raw_vo_in, 32)
            for m in range(C):
                for c in range(C):
                    k = VB + B * m
                    last = pe.matmul(pv[:, k:k + B], w_raw[:, 2, c, P * m:P * m + P], offs[:, 0, c, :],
                                     start=(c == 0), stop=(c == C - 1))
            last.then_inc(bias_mm, 1)
            pe.wait_ge(bias_ok, 1)
            keep_warm(16)
            pe.wait_ge(qk_ok, 2)
            pe.wait_ge(consts_ok, 2)
            def turn_y(j, c, bank):
                wait(pe, xhat2_ok, j + 1)
                for t in range(T):
                    last = pe.transpose(bank[:, P * t:P * t + P], xhat[:, t, P * c:P * c + P], ident[:, :])
                last.then_inc(x2_turned, 1)

            over_batches(pe, batch)

            pe.wait_ge(mlp_lo_ok, 2)

            def down(j, par, f):
                wait(pe, h_lo_ok, FT * j + f + 1)
                for t in range(T):
                    acc = sums[par][t // 2][:, D * (t % 2):D * (t % 2) + D]
                    for n, (a, b) in enumerate(TERMS):
                        last = pe.matmul(acc, (h_hi, h_lo)[a][:, f % HB, P * t:P * t + P], (w2_hi, w2_lo)[b][:, f, :],
                                         start=(f == 0 and n == 0 and t % 2 == 0), stop=(f == FT - 1 and n == 2),
                                         skip_group_check=True)
                last.then_inc(w2_mm, 1)

            def finish_attention(f):
                if f == 0:
                    pe.wait_ge(ym_lo_ok, 2)
                    turn_attn(B - 1, 0)
                if f == 2:
                    pe.wait_ge(at_lo_ok, 2 * B - 1)
                    project_out(B - 1, 0)
                if f == 3:
                    pe.wait_ge(x1_ok, 2 * B - 1)
                    turn_attn(B - 1, 1)
                if f == 4:
                    pe.wait_ge(at_lo_ok, 2 * B)
                    project_out(B - 1, 1)

            def mlp(j, par):
                for f in range(FT):
                    n = FT * j + f
                    if live(j, B):
                        if f == 0:
                            wait(pe, ym_lo_ok, 2 * j + 2)
                        wait(pe, h_ok, n - 1)
                        product(scores[f % 2][:, :], [parts((w1_hi, w1_lo), ALL, c, slice(P * f, P * f + P))
                                                      for c in range(C)],
                                [[y[:, c, :] for y in ym[par]] for c in range(C)]).then_inc(w1_mm, 1)
                    if f >= 2 and live(j, B):
                        down(j, par, f - 2)
                    if f < 2 and live(j - 1, B):
                        down(j - 1, 1 - par, FT - 2 + f)
                    if isinstance(j, int) and j == 0:
                        finish_attention(f)
                    if f in turn_at(j) and live(j + 1, B):
                        c = turn_at(j).index(f)
                        if isinstance(j, int) and j == 0:
                            wait(pe, x1_ok, 2 * B)
                        else:
                            wait(pe, ym_lo_ok, 2 * j + 1 + c)
                        turn_y(j + 1, c, (turn, work)[c])
                    if f == FT - 1 and live(j - 1, B):
                        wait(pe, y_ok, 2 * j)

            over_mlp_batches(pe, mlp)


_PRE = "L0_cond_"
_INS = ["x", "cond_1024"] + [_PRE + n for n in (
    "ln1_w", "ln1_b", "ln2_w", "ln2_b", "wq", "bq", "wk", "bk", "wv", "bv", "wo", "bo",
    "wt_attn", "bt_attn", "wt_ffn", "bt_ffn", "w1", "b1", "w2", "b2")]


def kernel(**inputs):
    import numpy as _np
    import concourse.bacc as _bacc
    from concourse import mybir as _mybir
    from concourse.bass_utils import run_bass_kernel_spmd as _run

    nc = _bacc.Bacc("TRN2", target_bir_lowering=False, num_devices=1)
    arrays, args = {}, []
    for name in _INS:
        a = _np.ascontiguousarray(inputs[name])
        arrays[f"in_{name}_dram"] = a
        args.append(nc.dram_tensor(f"in_{name}_dram", a.shape, _mybir.dt.from_np(a.dtype), kind="ExternalInput").ap())
    shape = inputs["x"].shape
    args.append(nc.dram_tensor("out_0_dram", shape, _mybir.dt.float32, kind="ExternalOutput").ap())
    cond_transformer_block(nc, *args)
    r = _run(nc, [arrays], core_ids=[0])
    return r.results[0]["out_0_dram"]
```
